# Optimizing a Trainium2 kernel written in Bass

```python
import numpy as np
import jax
import jax.numpy as jnp

def _softmax(x, axis=-1):
    return jax.nn.softmax(x, axis=axis)

def _gelu(x):
    return jax.nn.gelu(x, approximate=True)

def _silu(x):
    return jax.nn.silu(x)

def _sigmoid(x):
    return jax.nn.sigmoid(x)

def _layernorm(x, axis=-1, eps=1e-05):
    m = jnp.mean(x, axis=axis, keepdims=True)
    v = jnp.var(x, axis=axis, keepdims=True)
    return (x - m) / jnp.sqrt(v + eps)

def _scatter_add(tgt, idx, src, axis=0):
    return tgt.at[idx].add(src)

def _segment_sum(src, seg, n):
    return jax.ops.segment_sum(src, seg, n)
kernel_name = 'mk_gnn_preln_d2_gnn_r8_45eb65'

def setup_inputs(seed: int=0):
    np.random.seed(seed)
    _w = jnp.asarray

    def _rec_inputs():
        import jax
        import jax.numpy as jnp
        _gk = jax.random.key(seed)
        x = -0.000202 + 1 * jax.random.normal(jax.random.fold_in(_gk, 1), (12500, 64), jnp.float32)
        src = jax.random.randint(jax.random.fold_in(_gk, 2), (200000,), 0, 12500, jnp.int32)
        dst = jax.random.randint(jax.random.fold_in(_gk, 3), (200000,), 0, 12500, jnp.int32)
        _o = jnp.argsort(dst, stable=True)
        src = src[_o]
        dst = dst[_o]
        edge_attr_64 = -9.77346e-05 + 0.999888 * jax.random.normal(jax.random.fold_in(_gk, 12), (200000, 64), jnp.float32)
        return (x, src, dst, edge_attr_64)
    x, src, dst, edge_attr_64 = _rec_inputs()

    def _L0_gnn_setup():
        import jax, jax.numpy as jnp
        import numpy as np
        N = 12500
        E = 200000
        DIN = 64
        HID = 64
        OUT = 64

        def _sage_conv(x, src, dst, Wl, Wr, b):
            agg = jax.ops.segment_sum(x[src], dst, num_segments=N)
            cnt = jax.ops.segment_sum(jnp.ones((src.shape[0],), x.dtype), dst, num_segments=N)
            mean = agg / jnp.maximum(cnt, 1.0)[:, None]
            return mean @ Wl.T + b + x @ Wr.T
        key = jax.random.key(seed)
        ks = jax.random.split(key, 9)
        x = jax.random.normal(ks[0], (N, DIN), dtype=jnp.float32)
        edge_index = jax.random.randint(ks[1], (2, E), 0, N, dtype=jnp.int64)
        s1 = 1.0 / np.sqrt(DIN)
        s2 = 1.0 / np.sqrt(HID)
        W1l = jax.random.uniform(ks[2], (HID, DIN), jnp.float32, -s1, s1)
        W1r = jax.random.uniform(ks[3], (HID, DIN), jnp.float32, -s1, s1)
        b1 = jax.random.uniform(ks[4], (HID,), jnp.float32, -s1, s1)
        W2l = jax.random.uniform(ks[5], (OUT, HID), jnp.float32, -s2, s2)
        W2r = jax.random.uniform(ks[6], (OUT, HID), jnp.float32, -s2, s2)
        b2 = jax.random.uniform(ks[7], (OUT,), jnp.float32, -s2, s2)
        return {'x': x, 'edge_index': edge_index, 'W1l': W1l, 'W1r': W1r, 'b1': b1, 'W2l': W2l, 'W2r': W2r, 'b2': b2}
    _L0_gnn_all = _L0_gnn_setup()
    _L0_gnn_in = {k: v for k, v in _L0_gnn_all.items() if k in ('W1l', 'W1r', 'b1', 'W2l', 'W2r', 'b2')}
    del _L0_gnn_all

    def _L1_gnn_setup():
        import jax, jax.numpy as jnp
        import numpy as np
        N_NODES = 6250
        N_EDGES = 100000
        D = 64
        OUT_DIM = 64
        IN_DIM = 3 * D

        def _segment_mean(data, segment_ids, num_segments):
            sums = jax.ops.segment_sum(data, segment_ids, num_segments=num_segments, indices_are_sorted=True)
            counts = jax.ops.segment_sum(jnp.ones((data.shape[0],), dtype=data.dtype), segment_ids, num_segments=num_segments, indices_are_sorted=True)
            return sums / jnp.maximum(counts, 1.0)[:, None]
        key = jax.random.key(seed)
        k1, k2, k3, k4, k5, k6, k7, k8 = jax.random.split(key, 8)
        n_embed = jax.random.normal(k1, (N_NODES, D), dtype=jnp.float32)
        e_embed = jax.random.normal(k2, (N_EDGES, D), dtype=jnp.float32)
        senders = jnp.sort(jax.random.randint(k3, (N_EDGES,), 0, N_NODES))
        receivers = jax.random.randint(k4, (N_EDGES,), 0, N_NODES)
        W1 = jax.random.normal(k5, (IN_DIM, OUT_DIM), dtype=jnp.float32) / np.sqrt(IN_DIM)
        b1 = jnp.zeros((OUT_DIM,), dtype=jnp.float32)
        W2 = jax.random.normal(k6, (OUT_DIM, OUT_DIM), dtype=jnp.float32) / np.sqrt(OUT_DIM)
        b2 = jnp.zeros((OUT_DIM,), dtype=jnp.float32)
        return {'n_embed': n_embed, 'e_embed': e_embed, 'senders': senders, 'receivers': receivers, 'W1': W1, 'b1': b1, 'W2': W2, 'b2': b2}
    _L1_gnn_all = _L1_gnn_setup()
    _L1_gnn_in = {k: v for k, v in _L1_gnn_all.items() if k in ('W1', 'b1', 'W2', 'b2')}
    del _L1_gnn_all
    return {'x': x, 'src': src, 'dst': dst, 'edge_attr_64': edge_attr_64, 'L0_gnn_W1l': _L0_gnn_in['W1l'], 'L0_gnn_W1r': _L0_gnn_in['W1r'], 'L0_gnn_b1': _L0_gnn_in['b1'], 'L0_gnn_W2l': _L0_gnn_in['W2l'], 'L0_gnn_W2r': _L0_gnn_in['W2r'], 'L0_gnn_b2': _L0_gnn_in['b2'], 'L1_gnn_W1': _L1_gnn_in['W1'], 'L1_gnn_b1': _L1_gnn_in['b1'], 'L1_gnn_W2': _L1_gnn_in['W2'], 'L1_gnn_b2': _L1_gnn_in['b2']}

def reference(x, src, dst, edge_attr_64, L0_gnn_W1l, L0_gnn_W1r, L0_gnn_b1, L0_gnn_W2l, L0_gnn_W2r, L0_gnn_b2, L1_gnn_W1, L1_gnn_b1, L1_gnn_W2, L1_gnn_b2):
    import jax
    import jax.numpy as jnp

    def _L0_gnn_ref(x, edge_index, W1l, W1r, b1, W2l, W2r, b2):
        import jax, jax.numpy as jnp
        import numpy as np
        N = 12500
        E = 200000
        DIN = 64
        HID = 64
        OUT = 64

        def _sage_conv(x, src, dst, Wl, Wr, b):
            agg = jax.ops.segment_sum(x[src], dst, num_segments=N)
            cnt = jax.ops.segment_sum(jnp.ones((src.shape[0],), x.dtype), dst, num_segments=N)
            mean = agg / jnp.maximum(cnt, 1.0)[:, None]
            return mean @ Wl.T + b + x @ Wr.T
        src, dst = (edge_index[0], edge_index[1])
        h = jax.nn.relu(_sage_conv(x, src, dst, W1l, W1r, b1))
        out = _sage_conv(h, src, dst, W2l, W2r, b2)
        return out

    def _L1_gnn_ref(n_embed, e_embed, senders, receivers, W1, b1, W2, b2):
        import jax, jax.numpy as jnp
        import numpy as np
        N_NODES = 6250
        N_EDGES = 100000
        D = 64
        OUT_DIM = 64
        IN_DIM = 3 * D

        def _segment_mean(data, segment_ids, num_segments):
            sums = jax.ops.segment_sum(data, segment_ids, num_segments=num_segments, indices_are_sorted=True)
            counts = jax.ops.segment_sum(jnp.ones((data.shape[0],), dtype=data.dtype), segment_ids, num_segments=num_segments, indices_are_sorted=True)
            return sums / jnp.maximum(counts, 1.0)[:, None]
        inp = jnp.concatenate([n_embed[senders], n_embed[receivers], e_embed], axis=-1)
        h = jax.nn.relu(inp @ W1 + b1)
        msg = h @ W2 + b2
        return _segment_mean(msg, senders, n_embed.shape[0])
    edge_index = jnp.stack([src, dst])
    h = jnp.maximum(_layernorm(x, axis=-1), 0.0)
    x = x + _L0_gnn_ref(h, edge_index, L0_gnn_W1l, L0_gnn_W1r, L0_gnn_b1, L0_gnn_W2l, L0_gnn_W2r, L0_gnn_b2)
    h = jnp.maximum(_layernorm(x, axis=-1), 0.0)
    x = x + _L1_gnn_ref(h, edge_attr_64, src, dst, L1_gnn_W1, L1_gnn_b1, L1_gnn_W2, L1_gnn_b2)
    return x

_drawn_inputs = setup_inputs


def setup_inputs(seed=0):
    import zlib

    import numpy as np

    out = dict(_drawn_inputs(seed))
    spreads = {'L1_gnn_b1': (0.0, 0.1), 'L1_gnn_b2': (0.0, 0.1)}
    factors = {}
    for name, (base, spread) in spreads.items():
        noise = np.random.default_rng([zlib.crc32(name.encode()), seed]).standard_normal(out[name].shape)
        drawn = base * np.exp(spread * noise) if base else spread * noise
        out[name] = jnp.asarray(drawn.astype(out[name].dtype))
    for name, factor in factors.items():
        out[name] = (out[name] * factor).astype(out[name].dtype)
    return out
```

```python
from contextlib import ExitStack

import concourse.bass as bass
from concourse import mybir

P = 128
N = 12500
E = 200000
D = 64
D1 = D + 1
CH = 8
CE = CH * P
NCH = -(-E // CE)
FULL = E // CE
REST_P = (E - FULL * CE) // CH
W = P
W_SHIFT = 7
WINDOWS = N // W + 1
ROWS = N + P
NP_, NQ = 125, 4
NC_ = NP_ * NQ
NODE_CHUNKS = N // NC_
NR = NQ * D
TABLES = 4
EPS = 1e-5
assert NODE_CHUNKS * NC_ == N and NCH % 2 == 0 and NCH - FULL == 1 and REST_P * CH == E - FULL * CE

ALU = mybir.AluOpType
ACT = mybir.ActivationFunctionType
AX = mybir.AxisListType.X
F32 = mybir.dt.float32
I32 = mybir.dt.int32
U32 = mybir.dt.uint32


class Core:
    pass


def wait_alone(eng, sem, value):
    if not isinstance(value, int):
        value = eng.to_reg(value)
    eng.wait_ge(sem, 1)
    eng.wait_ge(sem, value)


def link(eng, ins, sem, value):
    ins.then_inc(sem, 1)
    eng.wait_ge(sem, value)


def node_rows(table):
    return table[0:N, :].rearrange("(c p q) d -> p c (q d)", p=NP_, q=NQ)


def setup(nc, ctx, k, io):
    def sb(name, shape, dt=F32):
        return ctx.enter_context(nc.sbuf_tensor(name, shape, dt))

    k.ident = sb("ident", [P, P])
    k.before = sb("before", [P, P])
    k.iota = sb("iota", [P, W])
    k.window_neg = sb("window_neg", [P, WINDOWS])
    k.window_pos = sb("window_pos", [P, WINDOWS])
    k.spare_row = sb("spare_row", [P, 1])
    k.conv_w = [[sb(f"conv{i}_{s}T", [D, P]) for s in "lr"] for i in (1, 2)]
    k.conv_b = [sb(f"conv{i}_b", [D, 1]) for i in (1, 2)]
    k.count_row = sb("count_row", [D1, D])
    k.edge_ends = sb("edge_ends", [D, 2 * D])
    k.edge_attr_w = sb("edge_attr_w", [P, 2, D])
    k.edge_b1 = sb("edge_b1", [NP_, D])
    k.edge_out = sb("edge_out", [D1, D1])
    k.src = sb("src_f", [P, NCH, CH])
    k.dst_rel = sb("dst_rel", [P, NCH, CH])
    k.win_row = sb("win_row", [1, 2 * NCH], I32)
    k.win_node = sb("win_node", [P, NCH])
    k.x = sb("x", [NP_, NODE_CHUNKS, NR])

    def dram(name, shape, dt=F32):
        return nc.dram_tensor(name, shape, dt).ap()

    k.h_table, k.g_table, k.a_table, k.b_table = (dram(n, [ROWS, D]) for n in ("h_table", "g_table", "a_table", "b_table"))
    k.sums = [dram(f"sums{i}", [ROWS, D1]) for i in range(TABLES)]
    k.src_pad = dram("src_pad", [NCH * CE], I32)
    k.dst_pad = dram("dst_pad", [NCH * CE], I32)
    windows = dram("windows", [2, NCH], I32)

    with ExitStack() as own:
        def tmp(name, shape, dt=F32):
            return own.enter_context(nc.sbuf_tensor(name, shape, dt))

        def sem(name):
            return own.enter_context(nc.semaphore(name))

        src_i = tmp("src_i", [P, NCH, CH], I32)
        dst_i = tmp("dst_i", [P, NCH, CH], I32)
        pad_i = tmp("pad_i", [1, NCH * CE - E], I32)
        zeros = tmp("zeros", [P, 10 * D1])
        ones = tmp("ones", [P, P])
        w_rows = tmp("w_rows", [D, 4, D])
        dst_chunks = tmp("dst_chunks", [NCH // 2, 2, CE], I32)
        least = tmp("least", [NCH // 2, 2], I32)
        most = tmp("most", [NCH // 2, 2], I32)
        count = tmp("count", [NCH // 2, 2], I32)
        base_i = tmp("base_i", [P, NCH], I32)
        base_f = tmp("base_f", [P, NCH])
        node = tmp("node", [P, 1])
        wt_ps = own.enter_context(nc.psum_tensor("wt_ps", [D, 4, D], F32))
        cleared, made, constants = sem("cleared"), sem("made"), sem("constants")
        w_landed, ids_landed, x_landed, pads_stored = sem("w_landed"), sem("ids_landed"), sem("x_landed"), sem("pads_stored")
        chunks_landed, windows_made, windows_stored = sem("chunks_landed"), sem("windows_made"), sem("windows_stored")
        base_landed, row_landed, zeros_stored = sem("base_landed"), sem("row_landed"), sem("zeros_stored")
        w_turned, step = sem("w_turned"), sem("step")
        block = own.enter_context(nc.Block())

        @block.sync
        def _(sp):
            sp.dma_start(k.x[:], node_rows_of_input(io["x"])).then_inc(x_landed, 16)
            for i, name in enumerate(("L0_gnn_W1l", "L0_gnn_W1r", "L0_gnn_W2l", "L0_gnn_W2r")):
                sp.dma_start(w_rows[:, i, :], io[name]).then_inc(w_landed, 16)
            for i, name in enumerate(("L0_gnn_b1", "L0_gnn_b2")):
                sp.dma_start(k.conv_b[i][:], io[name].rearrange("(d a) -> d a", a=1)).then_inc(w_landed, 16)
            w1 = io["L1_gnn_W1"]
            for i in range(2):
                sp.dma_start(k.edge_ends[:, i * D:(i + 1) * D], w1[i * D:(i + 1) * D, :]).then_inc(w_landed, 16)
            sp.dma_start(k.edge_b1[:], io["L1_gnn_b1"].rearrange("(a d) -> a d", a=1).to_broadcast([NP_, D])).then_inc(w_landed, 16)
            sp.wait_ge(cleared, 1)
            for i in range(2):
                sp.dma_start(k.edge_attr_w[i * D:(i + 1) * D, i, :], w1[2 * D:3 * D, :]).then_inc(w_landed, 16)
            sp.dma_start(k.edge_out[0:D, 0:D], io["L1_gnn_W2"]).then_inc(w_landed, 16)
            sp.dma_start(k.edge_out[D:D1, 0:D], io["L1_gnn_b2"].rearrange("(a d) -> a d", a=1)).then_inc(w_landed, 16)
            for name, to, pad in (("src", src_i, k.src_pad), ("dst", dst_i, k.dst_pad)):
                sp.dma_start(to[:, 0:FULL, :], io[name][0:FULL * CE].rearrange("(c p t) -> p c t", p=P, t=CH)).then_inc(ids_landed, 16)
                sp.dma_start(to[0:REST_P, FULL, :], io[name][FULL * CE:E].rearrange("(p t) -> p t", t=CH)).then_inc(ids_landed, 16)
                sp.dma_start(pad[0:E], io[name]).then_inc(pads_stored, 16)
                sp.dma_start(pad[E:NCH * CE].rearrange("(a e) -> a e", a=1), pad_i[:]).then_inc(pads_stored, 16)
            sp.wait_ge(pads_stored, 64)
            sp.dma_start(dst_chunks[:], k.dst_pad.rearrange("(c a e) -> c a e", a=2, e=CE)).then_inc(chunks_landed, 16)
            sp.wait_ge(windows_made, 1)
            for i, w in enumerate((least, count)):
                sp.dma_start(windows[i].rearrange("(c a) -> c a", a=2), w[:]).then_inc(windows_stored, 16)
            sp.wait_ge(windows_stored, 32)
            sp.dma_start(k.win_row[:], windows.rearrange("(o i) c -> o (i c)", o=1)).then_inc(row_landed, 16)
            sp.dma_start(base_i[:], windows[0:1, :].to_broadcast([P, NCH])).then_inc(base_landed, 16)
            sp.wait_ge(x_landed, 16)
            sp.wait_ge(w_landed, 16 * 13)
            sp.wait_ge(row_landed, 16)

        @block.scalar
        def _(act):
            act.wait_ge(cleared, 1)
            for table in (k.h_table, k.g_table, k.a_table, k.b_table):
                act.dma_start(table[N:ROWS, :], zeros[:, 0:D]).then_inc(zeros_stored, 16)
            for s in k.sums:
                act.dma_start(s[0:N, :].rearrange("(p a r) d -> p a (r d)", p=NP_, r=10),
                              zeros[0:NP_, :].unsqueeze(1).to_broadcast([NP_, N // NP_ // 10, 10 * D1])).then_inc(zeros_stored, 16)
                act.dma_start(s[N:ROWS, :], zeros[:, 0:D1]).then_inc(zeros_stored, 16)
            act.wait_ge(zeros_stored, 16 * (4 + 2 * TABLES))

        @block.gpsimd
        def _(pool):
            pool.iota(k.iota[:], [[1, W]], base=0, channel_multiplier=0, allow_small_or_imprecise_dtypes=True)
            pool.iota(k.window_neg[:], [[-W, WINDOWS]], base=0, channel_multiplier=0, allow_small_or_imprecise_dtypes=True)
            pool.iota(k.window_pos[:], [[W, WINDOWS]], base=0, channel_multiplier=0, allow_small_or_imprecise_dtypes=True)
            pool.iota(k.spare_row[:], [[0, 1]], base=N, channel_multiplier=1, allow_small_or_imprecise_dtypes=True)
            pool.iota(node[:], [[0, 1]], base=0, channel_multiplier=1, allow_small_or_imprecise_dtypes=True).then_inc(made, 1)
            pool.wait_ge(cleared, 1)
            pool.affine_select(out=k.ident[:], in_=k.ident[:], pattern=[[-1, P]], compare_op=ALU.not_equal, fill=1.0,
                               base=0, channel_multiplier=1).then_inc(constants, 1)
            pool.affine_select(out=k.before[:], in_=ones[:], pattern=[[-1, P]], compare_op=ALU.is_gt, fill=0.0,
                               base=0, channel_multiplier=1).then_inc(constants, 1)

        @block.tensor
        def _(pe):
            pe.wait_ge(constants, 2)
            pe.wait_ge(w_landed, 16 * 13)
            for i in range(4):
                mm = pe.transpose(wt_ps[:, i, :], w_rows[:, i, :], k.ident[0:D, 0:D])
            mm.then_inc(w_turned, 1)

        @block.vector
        def _(dve):
            dve.memset(zeros[:], 0.0)
            dve.memset(k.ident[:], 0.0)
            dve.memset(ones[:], 1.0)
            dve.memset(k.count_row[:], 0.0)
            dve.memset(k.edge_attr_w[:], 0.0)
            for i in range(2):
                for j in range(2):
                    dve.memset(k.conv_w[i][j][:], 0.0)
            link(dve, dve.memset(k.edge_out[:], 0.0), step, 1)
            dve.memset(k.count_row[D:D1, :], 1.0)
            dve.memset(k.edge_out[D:D1, D:D1], 1.0)
            dve.memset(src_i[:, FULL, :], N)
            dve.memset(dst_i[:, FULL, :], N)
            dve.memset(pad_i[:], N).then_inc(cleared, 1)
            dve.wait_ge(chunks_landed, 16)
            dve.tensor_reduce(least[:], dst_chunks[:], AX, ALU.min)
            link(dve, dve.tensor_reduce(most[:], dst_chunks[:], AX, ALU.max), step, 2)
            link(dve, dve.tensor_tensor(count[:], most[:], least[:], ALU.subtract), step, 3)
            link(dve, dve.tensor_scalar(count[:], count[:], W_SHIFT, None, ALU.arith_shift_right), step, 4)
            dve.tensor_scalar(count[:], count[:], 1, None, ALU.add).then_inc(windows_made, 1)
            dve.wait_ge(ids_landed, 64)
            dve.tensor_copy(k.src[:], src_i[:])
            dve.wait_ge(base_landed, 16)
            dve.wait_ge(made, 1)
            link(dve, dve.tensor_copy(base_f[:], base_i[:]), step, 5)
            dve.tensor_scalar(k.win_node[:], base_f[:], node[:, 0:1], None, ALU.add)
            dve.tensor_tensor(k.dst_rel[:], dst_i[:], base_f[:].unsqueeze(2).to_broadcast([P, NCH, CH]), ALU.subtract)
            dve.wait_ge(w_turned, 1)
            for i in range(2):
                for j in range(2):
                    dve.tensor_copy(k.conv_w[i][j][:, 0:D], wt_ps[:, 2 * i + j, :])


def node_rows_of_input(x):
    return x.rearrange("(c p q) d -> p c (q d)", p=NP_, q=NQ)


def norm_relu(nc, k, name, h, table):
    n = NODE_CHUNKS * NQ
    with ExitStack() as own:
        def tmp(s, shape):
            return own.enter_context(nc.sbuf_tensor(f"{name}_{s}", shape, F32))

        def sem(s):
            return own.enter_context(nc.semaphore(f"{name}_{s}"))

        square = tmp("square", [NP_, n, D])
        mean, var, root, rstd, fix = (tmp(s, [NP_, n]) for s in ("mean", "var", "root", "rstd", "fix"))
        var_ready, root_ready, h_ready, h_stored = sem("var_ready"), sem("root_ready"), sem("h_ready"), sem("h_stored")
        step = sem("step")
        block = own.enter_context(nc.Block())
        x3 = k.x[:].rearrange("p c (q d) -> p (c q) d", d=D)
        h3 = h[:].rearrange("p c (q d) -> p (c q) d", d=D)

        def wide(v):
            return v[:].unsqueeze(2).to_broadcast([NP_, n, D])

        @block.vector
        def _(dve):
            link(dve, dve.tensor_reduce(mean[:], x3, AX, ALU.add), step, 1)
            link(dve, dve.tensor_scalar(mean[:], mean[:], 1.0 / D, None, ALU.mult), step, 2)
            link(dve, dve.tensor_tensor(h3, x3, wide(mean), ALU.subtract), step, 3)
            link(dve, dve.tensor_tensor(square[:], h3, h3, ALU.mult), step, 4)
            link(dve, dve.tensor_reduce(var[:], square[:], AX, ALU.add), step, 5)
            dve.tensor_scalar(var[:], var[:], 1.0 / D, EPS, ALU.mult, ALU.add).then_inc(var_ready, 1)
            dve.wait_ge(root_ready, 1)
            link(dve, dve.reciprocal(rstd[:], root[:]), step, 6)
            link(dve, dve.tensor_tensor(fix[:], rstd[:], rstd[:], ALU.mult), step, 7)
            link(dve, dve.tensor_tensor(fix[:], fix[:], var[:], ALU.mult), step, 8)
            link(dve, dve.tensor_scalar(fix[:], fix[:], -0.5, 1.5, ALU.mult, ALU.add), step, 9)
            link(dve, dve.tensor_tensor(rstd[:], rstd[:], fix[:], ALU.mult), step, 10)
            dve.scalar_tensor_tensor(h3, h3, 0.0, wide(rstd), ALU.max, ALU.mult).then_inc(h_ready, 1)

        @block.scalar
        def _(act):
            act.wait_ge(var_ready, 1)
            act.activation(root[:], var[:], ACT.Sqrt).then_inc(root_ready, 1)

        if table is not None:
            @block.sync
            def _(sp):
                sp.wait_ge(h_ready, 1)
                sp.dma_start(node_rows(table), h[:]).then_inc(h_stored, 16)
                sp.wait_ge(h_stored, 16)


def turn_rows(nc, k, h, h_t):
    with ExitStack() as own:
        stage = own.enter_context(nc.sbuf_tensor("turn_stage", [NP_, NR], F32))
        turned = own.enter_context(nc.psum_tensor("turn_ps", [D, NQ, P], F32))
        staged, turned_ready, kept = (own.enter_context(nc.semaphore(f"turn_{s}")) for s in ("staged", "ready", "kept"))
        block = own.enter_context(nc.Block())

        @block.scalar
        def _(act):
            with act.Fori(0, NODE_CHUNKS) as c:
                act.copy(stage[:], h[:, bass.ds(c, 1), :].rearrange("p c r -> p (c r)")).then_inc(staged, 1)
                act.wait_ge(turned_ready, c + 1)
                act.copy(h_t[:, bass.ds(c * NC_, NC_)].rearrange("d (p q) -> d q p", q=NQ), turned[:, :, 0:NP_]).then_inc(kept, 1)

        @block.tensor
        def _(pe):
            with pe.Fori(0, NODE_CHUNKS) as c:
                wait_alone(pe, staged, c + 1)
                for q in range(NQ):
                    mm = pe.transpose(turned[:, q, 0:NP_], stage[:, q * D:(q + 1) * D], k.ident[0:NP_, 0:NP_])
                mm.then_inc(turned_ready, 1)


def sum_by_dst(nc, k, name, table, acc):
    with ExitStack() as own:
        def tmp(s, shape, dt=F32):
            return own.enter_context(nc.sbuf_tensor(f"{name}_{s}", shape, dt))

        def sem(s):
            return own.enter_context(nc.semaphore(f"{name}_{s}"))

        rows = tmp("rows", [P, 2, CH, D1])
        index = [tmp(f"index{h}", [P, CH], U32) for h in range(2)]
        one_hot = tmp("one_hot", [P, 2, CH, W])
        sums = [own.enter_context(nc.psum_tensor(f"{name}_sums{h}", [P, 512], F32)) for h in range(2)]
        ones_set = sem("ones_set")
        index_ready = [sem(f"index_ready{h}") for h in range(2)]
        landed = [sem(f"landed{h}") for h in range(2)]
        rows_used = [sem(f"rows_used{h}") for h in range(2)]
        hot_ready, window_done, added = sem("hot_ready"), sem("window_done"), sem("added")
        block = own.enter_context(nc.Block())

        @block.gpsimd
        def _(pool):
            pool.wait_ge(ones_set, 1)
            with pool.Fori(0, NCH // 2) as i:
                for h in range(2):
                    wait_alone(pool, index_ready[h], i + 1)
                    for t in range(CH):
                        pool.indirect_dma_start(rows[:, h, t, 0:D], None, table,
                                                bass.IndirectOffsetOnAxis(ap=index[h][:, t:t + 1], axis=0)).then_inc(landed[h], 16)

        @block.scalar
        def _(act):
            def put_index(c, h):
                act.copy(index[h][:], k.src[:, bass.ds(c, 1), :].rearrange("p c t -> p (c t)")).then_inc(index_ready[h], 1)

            for h in range(2):
                put_index(h, h)
            with act.Fori(1, NCH // 2) as i:
                for h in range(2):
                    act.wait_ge(rows_used[h], i)
                    put_index(2 * i + h, h)

        @block.tensor
        def _(pe):
            windows = pe.alloc_register(f"{name}_pe_windows")
            pe.reg_mov(windows, 0)
            with pe.Fori(0, NCH // 2) as i:
                for h in range(2):
                    count = pe.value_load(k.win_row[0:1, bass.ds(NCH + 2 * i + h, 1)], min_val=1, max_val=WINDOWS)
                    wait_alone(pe, landed[h], 16 * CH * (i + 1))
                    with pe.Fori(0, count):
                        pe.reg_add(windows, windows, 1)
                        pe.wait_ge(hot_ready, pe.snap(windows, min_val=1, max_val=NCH * WINDOWS))
                        for t in range(CH):
                            mm = pe.matmul(sums[h][0:D1, 0:W], rows[:, h, t, :], one_hot[:, h, t, :], start=(t == 0), stop=(t == CH - 1))
                        mm.then_inc(window_done, 1)

        @block.vector
        def _(dve):
            dve.memset(rows[:], 1.0).then_inc(ones_set, 1)
            dve.memset(acc[:], 0.0).then_inc(added, 1)
            done = dve.alloc_register(f"{name}_dve_done")
            first = dve.alloc_register(f"{name}_dve_first")
            dve.reg_mov(done, 0)
            dve.reg_mov(first, 0)

            def make_hot(c, h, w):
                for t in range(CH):
                    hot = dve.tensor_scalar(one_hot[:, h, t, :], k.iota[:], k.dst_rel[:, bass.ds(c, 1), t], k.window_neg[:, bass.ds(w, 1)],
                                            ALU.subtract, ALU.is_equal)
                hot.then_inc(hot_ready, 1)

            def add_window(h):
                dve.reg_add(done, done, 1)
                windows = dve.snap(done, min_val=1, max_val=NCH * WINDOWS)
                part = acc[:, bass.ds(dve.snap(first, min_val=0, max_val=N), W)]
                dve.wait_ge(window_done, windows)
                dve.wait_ge(added, windows)
                dve.tensor_tensor(part, part, sums[h][0:D1, 0:W], ALU.add).then_inc(added, 1)

            def chunk(c, h, before):
                count = dve.value_load(k.win_row[0:1, bass.ds(c + NCH, 1)], min_val=1, max_val=WINDOWS)
                base = dve.value_load(k.win_row[0:1, bass.ds(c, 1)], min_val=0, max_val=N)
                make_hot(c, h, 0)
                if before:
                    add_window(1 - h)
                    dve.sem_inc(rows_used[1 - h], 1)
                dve.reg_mov(first, base)
                with dve.If(count > 1):
                    with dve.Fori(1, count) as w:
                        add_window(h)
                        make_hot(c, h, w)
                        dve.reg_add(first, first, W)

            chunk(0, 0, False)
            with dve.Fori(0, NCH // 2 - 1) as i:
                chunk(2 * i + 1, 1, True)
                chunk(2 * i + 2, 0, True)
            chunk(NCH - 1, 1, True)
            add_window(1)


def convolve(nc, k, name, step, acc, h_t, table):
    first = step == 0
    with ExitStack() as own:
        def tmp(s, shape):
            return own.enter_context(nc.sbuf_tensor(f"{name}_{s}", shape, F32))

        def psum(s, shape):
            return own.enter_context(nc.psum_tensor(f"{name}_{s}", shape, F32))

        def sem(s):
            return own.enter_context(nc.semaphore(f"{name}_{s}"))

        inv, mean, made, rows = tmp("inv", [D, NC_]), tmp("mean", [D, NC_]), tmp("made", [D, NC_]), tmp("rows", [NP_, NR])
        count_ps, conv_ps, rows_ps = psum("count_ps", [D, 512]), psum("conv_ps", [P, 512]), psum("rows_ps", [P, 512])
        counted, mean_ready, summed, made_ready, turned, rows_ready, stored, step_done, kept = (
            sem(s) for s in ("counted", "mean_ready", "summed", "made_ready", "turned", "rows_ready", "stored", "step_done", "kept"))
        block = own.enter_context(nc.Block())

        @block.tensor
        def _(pe):
            w_l, w_r = k.conv_w[step]
            with pe.Fori(0, NODE_CHUNKS) as c:
                nodes = bass.ds(c * NC_, NC_)
                pe.matmul(count_ps[:, 0:NC_], k.count_row[:], acc[:, nodes], start=True, stop=True).then_inc(counted, 1)
                wait_alone(pe, mean_ready, c + 1)
                pe.matmul(conv_ps[:, 0:NC_], w_l[:], mean[:], start=True, stop=False)
                pe.matmul(conv_ps[:, 0:NC_], w_r[:], h_t[:, nodes], start=False, stop=True).then_inc(summed, 1)
                wait_alone(pe, made_ready, c + 1)
                for q in range(NQ):
                    mm = pe.transpose(rows_ps[0:NP_, q * D:(q + 1) * D], made[:, bass.ds(q, NP_, step=NQ)], k.ident[0:D, 0:D])
                mm.then_inc(turned, 1)
                pe.wait_ge(rows_ready, c + 1)

        @block.vector
        def _(dve):
            with dve.Fori(0, NODE_CHUNKS) as c:
                dve.wait_ge(counted, c + 1)
                link(dve, dve.tensor_scalar(inv[:], count_ps[:, 0:NC_], 1.0, None, ALU.max), step_done, 2 * c + 1)
                link(dve, dve.reciprocal(inv[:], inv[:]), step_done, 2 * c + 2)
                dve.tensor_tensor(mean[:], acc[0:D, bass.ds(c * NC_, NC_)], inv[:], ALU.mult).then_inc(mean_ready, 1)
                dve.wait_ge(turned, c + 1)
                if first:
                    dve.tensor_copy(rows[:], rows_ps[0:NP_, 0:NR]).then_inc(rows_ready, 1)
                    dve.wait_ge(stored, 16 * (c + 1))
                else:
                    x = k.x[:, bass.ds(c, 1), :].rearrange("p c r -> p (c r)")
                    dve.tensor_tensor(x, x, rows_ps[0:NP_, 0:NR], ALU.add).then_inc(rows_ready, 1)

        @block.scalar
        def _(act):
            with act.Fori(0, NODE_CHUNKS) as c:
                act.wait_ge(summed, c + 1)
                act.activation(made[:], conv_ps[0:D, 0:NC_], ACT.Relu if first else ACT.Identity, bias=k.conv_b[step][:, 0:1]).then_inc(made_ready, 1)
                if first:
                    act.wait_ge(made_ready, c + 1)
                    link(act, act.copy(h_t[:, bass.ds(c * NC_, NC_)], made[:]), kept, c + 1)

        if first:
            @block.sync
            def _(sp):
                out = node_rows(table)
                with sp.Fori(0, NODE_CHUNKS) as c:
                    sp.wait_ge(rows_ready, c + 1)
                    sp.dma_start(out[:, bass.ds(c, 1), :].rearrange("p c r -> p (c r)"), rows[:]).then_inc(stored, 16)
                sp.wait_ge(stored, 16 * NODE_CHUNKS)


def edge_tables(nc, k, h):
    with ExitStack() as own:
        def tmp(s, shape):
            return own.enter_context(nc.sbuf_tensor(f"ends_{s}", shape, F32))

        def sem(s):
            return own.enter_context(nc.semaphore(f"ends_{s}"))

        stage, h_t = tmp("stage", [NP_, NR]), tmp("h_t", [D, NQ, NP_])
        a_rows, b_rows = tmp("a", [NP_, NQ, D]), tmp("b", [NP_, NQ, D])
        turn_ps = own.enter_context(nc.psum_tensor("ends_turn_ps", [D, NQ, P], F32))
        ends_ps = own.enter_context(nc.psum_tensor("ends_ps", [P, NQ, 2 * D], F32))
        staged, turned, h_t_ready, product, rows_ready, a_stored, b_stored = (
            sem(s) for s in ("staged", "turned", "h_t_ready", "product", "rows_ready", "a_stored", "b_stored"))
        block = own.enter_context(nc.Block())

        @block.scalar
        def _(act):
            with act.Fori(0, NODE_CHUNKS) as c:
                act.copy(stage[:], h[:, bass.ds(c, 1), :].rearrange("p c r -> p (c r)")).then_inc(staged, 1)
                act.wait_ge(turned, c + 1)
                act.copy(h_t[:], turn_ps[:, :, 0:NP_]).then_inc(h_t_ready, 1)
                act.wait_ge(product, c + 1)

        @block.tensor
        def _(pe):
            with pe.Fori(0, NODE_CHUNKS) as c:
                wait_alone(pe, staged, c + 1)
                for q in range(NQ):
                    mm = pe.transpose(turn_ps[:, q, 0:NP_], stage[:, q * D:(q + 1) * D], k.ident[0:NP_, 0:NP_])
                mm.then_inc(turned, 1)
                wait_alone(pe, h_t_ready, c + 1)
                for q in range(NQ):
                    mm = pe.matmul(ends_ps[0:NP_, q, :], h_t[:, q, :], k.edge_ends[:], start=True, stop=True)
                mm.then_inc(product, 1)
                pe.wait_ge(rows_ready, c + 1)

        @block.vector
        def _(dve):
            with dve.Fori(0, NODE_CHUNKS) as c:
                dve.wait_ge(product, c + 1)
                dve.tensor_copy(a_rows[:], ends_ps[0:NP_, :, 0:D])
                dve.tensor_tensor(b_rows[:], ends_ps[0:NP_, :, D:2 * D], k.edge_b1[:].unsqueeze(1).to_broadcast([NP_, NQ, D]),
                                  ALU.add).then_inc(rows_ready, 1)
                dve.wait_ge(a_stored, 16 * (c + 1))
                dve.wait_ge(b_stored, 16 * (c + 1))

        @block.sync
        def _(sp):
            a_out, b_out = node_rows(k.a_table), node_rows(k.b_table)
            with sp.Fori(0, NODE_CHUNKS) as c:
                sp.wait_ge(rows_ready, c + 1)
                sp.dma_start(a_out[:, bass.ds(c, 1), :].rearrange("p c r -> p (c r)"), a_rows[:].rearrange("p q d -> p (q d)")).then_inc(a_stored, 16)
                sp.dma_start(b_out[:, bass.ds(c, 1), :].rearrange("p c r -> p (c r)"), b_rows[:].rearrange("p q d -> p (q d)")).then_inc(b_stored, 16)
            sp.wait_ge(a_stored, 16 * NODE_CHUNKS)
            sp.wait_ge(b_stored, 16 * NODE_CHUNKS)


def edges(nc, k, edge_attr):
    with ExitStack() as own:
        def tmp(s, shape, dt=F32):
            return own.enter_context(nc.sbuf_tensor(f"edge_{s}", shape, dt))

        def psum(s, shape):
            return own.enter_context(nc.psum_tensor(f"edge_{s}", shape, F32))

        def sem(s):
            return own.enter_context(nc.semaphore(f"edge_{s}"))

        def pair(make, s, *a):
            return [make(f"{s}{h}", *a) for h in range(2)]

        rows, index = pair(tmp, "rows", [P, CH, D]), pair(tmp, "index", [P, CH], U32)
        attr, b_win = pair(tmp, "attr", [P, CH * D]), pair(tmp, "b_win", [W, D])
        src_row, dst_row = pair(tmp, "src_row", [P, CE], I32), pair(tmp, "dst_row", [P, CE], I32)
        hot_t, same = pair(tmp, "hot_t", [W, CH, P]), pair(tmp, "same", [P, CH, P])
        hidden, out_rows, out_index = pair(tmp, "hidden", [P, CH, D1]), pair(tmp, "out_rows", [P, CH, D1]), pair(tmp, "out_index", [P, CH], U32)
        attr_t = tmp("attr_t", [P, CH // 2, P])
        earlier, repeats, away, target = tmp("earlier", [P, CH, P]), tmp("repeats", [P, CH]), tmp("away", [P, CH]), tmp("target", [P, CH])
        hidden_ps = pair(psum, "hidden_ps", [P, CH, D])
        attr_ps, same_ps = psum("attr_ps", [P, CH // 2, P]), pair(psum, "same_ps", [P, CH // 2, P])
        index_ready, landed, loaded, b_landed, added = (pair(sem, s) for s in ("index_ready", "landed", "loaded", "b_landed", "added"))
        ones_set, hot_ready, window_done, attr_turned, attr_ready, relu_done, same_done, out_ready, step_done = (
            sem(s) for s in ("ones_set", "hot_ready", "window_done", "attr_turned", "attr_ready", "relu_done", "same_done", "out_ready", "step_done"))
        scattered = [sem(f"scattered{i}") for i in range(TABLES)]
        block = own.enter_context(nc.Block())
        PER = CH // TABLES

        def windows_of(eng, c):
            return eng.value_load(k.win_row[0:1, bass.ds(c + NCH, 1)], min_val=1, max_val=WINDOWS)

        def by_chunks(eng, body):
            body(0, 0, 0, early=True)
            body(1, 1, 0, early=True)
            with eng.Fori(1, NCH // 2 - 1) as i:
                body(2 * i, 0, i)
                body(2 * i + 1, 1, i)
            body(NCH - 2, 0, NCH // 2 - 1, late=True)
            body(NCH - 1, 1, NCH // 2 - 1, late=True)

        @block.sync
        def _(sp):
            b_windows = [sp.alloc_register(f"edge_sp_windows{h}") for h in range(2)]
            first = sp.alloc_register("edge_sp_first")
            every = sp.alloc_register("edge_sp_every")
            sp.reg_mov(every, 0)
            sp.wait_ge(ones_set, 1)

            def load_window(h):
                at = sp.snap(first, min_val=0, max_val=N)
                sp.dma_start(b_win[h][:], k.b_table[bass.ds(at, W), :]).then_inc(b_landed[h], 16)
                sp.reg_add(every, every, 1)

            def body(c, h, used, early=False, late=False):
                count = windows_of(sp, c)
                base = sp.value_load(k.win_row[0:1, bass.ds(c, 1)], min_val=0, max_val=N)
                if not early:
                    sp.wait_ge(added[h], used)
                if late and h == 1:
                    sp.dma_start(attr[h][0:REST_P, :], edge_attr[FULL * CE:E, :].rearrange("(p t) d -> p (t d)", t=CH)).then_inc(loaded[h], 16)
                else:
                    sp.dma_start(attr[h][:], edge_attr.rearrange("(p t) d -> p (t d)", t=CH)[bass.ds(c * P, P), :]).then_inc(loaded[h], 16)
                for row, pad in ((src_row, k.src_pad), (dst_row, k.dst_pad)):
                    sp.dma_start(row[h][:], pad.rearrange("(c e) -> c e", e=CE)[bass.ds(c, 1), :].to_broadcast([P, CE])).then_inc(loaded[h], 16)
                sp.reg_mov(first, base)
                load_window(h)
                with sp.If(count > 1):
                    with sp.Fori(1, count):
                        sp.wait_ge(window_done, sp.snap(every, min_val=1, max_val=NCH * WINDOWS))
                        sp.reg_add(first, first, W)
                        load_window(h)

            by_chunks(sp, body)

        @block.gpsimd
        def _(pool):
            def gather(h, used):
                wait_alone(pool, index_ready[h], used + 1)
                for t in range(CH):
                    pool.indirect_dma_start(rows[h][:, t, :], None, k.a_table,
                                            bass.IndirectOffsetOnAxis(ap=index[h][:, t:t + 1], axis=0)).then_inc(landed[h], 16)

            def scatter(c, h, early=False):
                pool.wait_ge(out_ready, c + 1)
                for t in range(CH):
                    s = t % TABLES
                    if not (early and t < TABLES):
                        wait_alone(pool, scattered[s], 16 * (c * PER + t // TABLES))
                    pool.indirect_dma_start(k.sums[s], bass.IndirectOffsetOnAxis(ap=out_index[h][:, t:t + 1], axis=0),
                                            out_rows[h][:, t, :], None, compute_op=ALU.add).then_inc(scattered[s], 16)

            gather(0, 0)
            gather(1, 0)
            scatter(0, 0, early=True)
            with pool.Fori(1, NCH // 2) as i:
                gather(0, i)
                scatter(2 * i - 1, 1)
                gather(1, i)
                scatter(2 * i, 0)
            scatter(NCH - 1, 1)
            for s in range(TABLES):
                pool.wait_ge(scattered[s], 16 * PER * NCH)

        @block.tensor
        def _(pe):
            windows = pe.alloc_register("edge_pe_windows")
            half_windows = [pe.alloc_register(f"edge_pe_windows{h}") for h in range(2)]
            for r in (windows, *half_windows):
                pe.reg_mov(r, 0)

            def body(c, h, used, early=False, late=False):
                count = windows_of(pe, c)
                wait_alone(pe, loaded[h], 48 * (used + 1))
                for j in range(CH // 2):
                    mm = pe.transpose(attr_ps[:, j, :], attr[h][:, j * P:(j + 1) * P], k.ident[:])
                mm.then_inc(attr_turned, 1)
                pe.wait_ge(attr_ready, c + 1)
                if not early:
                    pe.wait_ge(added[h], used)
                for t in range(CH):
                    pe.matmul(hidden_ps[h][:, t, :], attr_t[:, t // 2, :], k.edge_attr_w[:, t % 2, :], start=(t == 0), stop=False, skip_group_check=True)
                with pe.Fori(0, count):
                    for r in (windows, half_windows[h]):
                        pe.reg_add(r, r, 1)
                    every, half = (pe.snap(r, min_val=1, max_val=NCH * WINDOWS) for r in (windows, half_windows[h]))
                    pe.wait_ge(hot_ready, every)
                    wait_alone(pe, b_landed[h], half * 16)
                    for t in range(CH):
                        mm = pe.matmul(hidden_ps[h][:, t, :], hot_t[h][:, t, :], b_win[h][:], start=False, stop=(t == CH - 1), skip_group_check=True)
                    mm.then_inc(window_done, 1)
                pe.wait_ge(relu_done, c + 1)
                if not (early and h == 0):
                    pe.wait_ge(out_ready, c)
                for t in range(CH):
                    mm = pe.matmul(same_ps[t // TABLES][:, t % TABLES, 0:D1], same[h][:, t, :], hidden[h][:, t, :], start=True, stop=True)
                mm.then_inc(same_done, 1)

            by_chunks(pe, body)

        @block.scalar
        def _(act):
            def put_index(c, h):
                act.copy(index[h][:], k.src[:, bass.ds(c, 1), :].rearrange("p c t -> p (c t)")).then_inc(index_ready[h], 1)

            for h in range(2):
                put_index(h, h)

            def body(c, h, used, early=False, late=False):
                act.wait_ge(attr_turned, c + 1)
                act.copy(attr_t[:], attr_ps[:]).then_inc(attr_ready, 1)
                act.wait_ge(added[h], used + 1)
                act.activation(hidden[h][:, :, 0:D], hidden[h][:, :, 0:D], ACT.Relu).then_inc(relu_done, 1)
                if not late:
                    put_index(c + 2, h)
                act.wait_ge(same_done, c + 1)
                if not early:
                    for s in range(TABLES):
                        act.wait_ge(scattered[s], 16 * PER * (c - 1))
                for g in range(2):
                    last = act.copy(out_rows[h][:, g * TABLES:(g + 1) * TABLES, :], same_ps[g][:, :, 0:D1])
                last.then_inc(out_ready, 1)

            by_chunks(act, body)

        @block.vector
        def _(dve):
            for h in range(2):
                dve.memset(hidden[h][:], 1.0)
            link(dve, dve.memset(attr[1][:], 0.0), ones_set, 1)
            done = dve.alloc_register("edge_dve_done")
            dve.reg_mov(done, 0)

            def make_hot(c, h, w):
                dve.tensor_scalar(hot_t[h][:], dst_row[h][:].rearrange("n (p t) -> n t p", t=CH), k.win_node[:, bass.ds(c, 1)],
                                  k.window_pos[:, bass.ds(w, 1)], ALU.subtract, ALU.is_equal).then_inc(hot_ready, 1)

            def make(c, h, used, early=False):
                count = windows_of(dve, c)
                dve.wait_ge(loaded[h], 48 * (used + 1))
                if not early:
                    dve.wait_ge(same_done, c - 1)
                for t in range(CH):
                    dve.tensor_scalar(same[h][:, t, :], src_row[h][:].rearrange("n (p t) -> n t p", t=CH)[:, t, :], k.src[:, bass.ds(c, 1), t], None, ALU.is_equal)
                make_hot(c, h, 0)
                dve.wait_ge(hot_ready, dve.snap(done, min_val=0, max_val=NCH * WINDOWS) + 1)
                link(dve, dve.tensor_tensor(earlier[:], same[h][:], k.before[:].unsqueeze(1).to_broadcast([P, CH, P]), ALU.mult), step_done, 4 * c + 1)
                dve.tensor_reduce(repeats[:], earlier[:], AX, ALU.max)
                src = k.src[:, bass.ds(c, 1), :].rearrange("p c t -> p (c t)")
                link(dve, dve.tensor_scalar(away[:], src, -1.0, k.spare_row[:, 0:1], ALU.mult, ALU.add), step_done, 4 * c + 2)
                link(dve, dve.tensor_tensor(away[:], away[:], repeats[:], ALU.mult), step_done, 4 * c + 3)
                link(dve, dve.tensor_tensor(target[:], away[:], src, ALU.add), step_done, 4 * c + 4)
                if not early:
                    for s in range(TABLES):
                        dve.wait_ge(scattered[s], 16 * PER * (c - 1))
                dve.tensor_copy(out_index[h][:], target[:])
                with dve.If(count > 1):
                    with dve.Fori(1, count) as w:
                        dve.reg_add(done, done, 1)
                        dve.wait_ge(window_done, dve.snap(done, min_val=1, max_val=NCH * WINDOWS))
                        make_hot(c, h, w)

            def add(c, h, used):
                dve.reg_add(done, done, 1)
                windows = dve.snap(done, min_val=1, max_val=NCH * WINDOWS)
                dve.wait_ge(landed[h], 16 * CH * (used + 1))
                dve.wait_ge(window_done, windows)
                dve.tensor_tensor(hidden[h][:, :, 0:D], hidden_ps[h][:], rows[h][:], ALU.add).then_inc(added[h], 1)

            last = NCH // 2 - 1
            make(0, 0, 0, early=True)
            add(0, 0, 0)
            make(1, 1, 0, early=True)
            with dve.Fori(1, last + 1) as i:
                add(2 * i - 1, 1, i - 1)
                make(2 * i, 0, i)
                add(2 * i, 0, i)
                make(2 * i + 1, 1, i)
            add(NCH - 1, 1, last)


def finish(nc, k, out):
    with ExitStack() as own:
        def tmp(s, shape):
            return own.enter_context(nc.sbuf_tensor(f"fin_{s}", shape, F32))

        def sem(s):
            return own.enter_context(nc.semaphore(f"fin_{s}"))

        parts, total, total_t = tmp("parts", [NP_, TABLES, NQ * D1]), tmp("total", [NP_, NQ * D1]), tmp("total_t", [D1, NQ, NP_])
        inv, rows = tmp("inv", [NP_, NQ]), tmp("rows", [NP_, NQ, D])
        turn_ps = own.enter_context(nc.psum_tensor("fin_turn_ps", [P, NQ, P], F32))
        out_ps = own.enter_context(nc.psum_tensor("fin_out_ps", [P, NQ, P], F32))
        landed, total_ready, turned, t_ready, product, rows_ready, stored, step_done = (
            sem(s) for s in ("landed", "total_ready", "turned", "t_ready", "product", "rows_ready", "stored", "step_done"))
        block = own.enter_context(nc.Block())

        @block.sync
        def _(sp):
            out_v = node_rows_of_input(out)

            def load(c):
                for i in range(TABLES):
                    sp.dma_start(parts[:, i, :], node_rows(k.sums[i])[:, bass.ds(c, 1), :].rearrange("p c r -> p (c r)")).then_inc(landed, 16)

            load(0)
            with sp.Fori(0, NODE_CHUNKS - 1) as c:
                sp.wait_ge(total_ready, c + 1)
                load(c + 1)
                sp.wait_ge(rows_ready, c + 1)
                sp.dma_start(out_v[:, bass.ds(c, 1), :].rearrange("p c r -> p (c r)"), rows[:].rearrange("p q d -> p (q d)")).then_inc(stored, 16)
            sp.wait_ge(rows_ready, NODE_CHUNKS)
            sp.dma_start(out_v[:, NODE_CHUNKS - 1, :], rows[:].rearrange("p q d -> p (q d)")).then_inc(stored, 16)
            sp.wait_ge(stored, 16 * NODE_CHUNKS)

        @block.vector
        def _(dve):
            with dve.Fori(0, NODE_CHUNKS) as c:
                dve.wait_ge(landed, 16 * TABLES * (c + 1))
                dve.tensor_reduce(total[:], parts[:].rearrange("p i m -> p m i"), AX, ALU.add).then_inc(total_ready, 1)
                dve.wait_ge(product, c + 1)
                link(dve, dve.tensor_scalar(inv[:].unsqueeze(2), out_ps[0:NP_, :, D:D1], 1.0, None, ALU.max), step_done, 3 * c + 1)
                link(dve, dve.reciprocal(inv[:], inv[:]), step_done, 3 * c + 2)
                link(dve, dve.tensor_tensor(rows[:], out_ps[0:NP_, :, 0:D], inv[:].unsqueeze(2).to_broadcast([NP_, NQ, D]), ALU.mult), step_done, 3 * c + 3)
                dve.tensor_tensor(rows[:], rows[:], k.x[:, bass.ds(c, 1), :].rearrange("p c (q d) -> p (c q) d", d=D), ALU.add).then_inc(rows_ready, 1)
                dve.wait_ge(stored, 16 * (c + 1))

        @block.tensor
        def _(pe):
            with pe.Fori(0, NODE_CHUNKS) as c:
                wait_alone(pe, total_ready, c + 1)
                for q in range(NQ):
                    mm = pe.transpose(turn_ps[0:D1, q, 0:NP_], total[:, q * D1:(q + 1) * D1], k.ident[0:NP_, 0:NP_])
                mm.then_inc(turned, 1)
                wait_alone(pe, t_ready, c + 1)
                for q in range(NQ):
                    mm = pe.matmul(out_ps[0:NP_, q, 0:D1], total_t[:, q, :], k.edge_out[:], start=True, stop=True)
                mm.then_inc(product, 1)
                pe.wait_ge(rows_ready, c + 1)

        @block.scalar
        def _(act):
            with act.Fori(0, NODE_CHUNKS) as c:
                act.wait_ge(turned, c + 1)
                act.copy(total_t[:], turn_ps[0:D1, :, 0:NP_]).then_inc(t_ready, 1)
                act.wait_ge(product, c + 1)


def program(nc, io, out):
    k = Core()
    with ExitStack() as ctx:
        setup(nc, ctx, k, io)
        with ExitStack() as conv:
            acc = conv.enter_context(nc.sbuf_tensor("acc", [D1, ROWS], F32))
            h_t = conv.enter_context(nc.sbuf_tensor("h_t", [D, N], F32))
            with nc.sbuf_tensor("h0", [NP_, NODE_CHUNKS, NR], F32) as h:
                norm_relu(nc, k, "norm0", h, k.h_table)
                turn_rows(nc, k, h, h_t)
            sum_by_dst(nc, k, "agg1", k.h_table, acc)
            convolve(nc, k, "conv1", 0, acc, h_t, k.g_table)
            sum_by_dst(nc, k, "agg2", k.g_table, acc)
            convolve(nc, k, "conv2", 1, acc, h_t, None)
        with nc.sbuf_tensor("h1", [NP_, NODE_CHUNKS, NR], F32) as h:
            norm_relu(nc, k, "norm1", h, None)
            edge_tables(nc, k, h)
        edges(nc, k, io["edge_attr_64"])
        finish(nc, k, out)


INS = ["x", "src", "dst", "edge_attr_64", "L0_gnn_W1l", "L0_gnn_W1r", "L0_gnn_b1", "L0_gnn_W2l", "L0_gnn_W2r", "L0_gnn_b2",
       "L1_gnn_W1", "L1_gnn_b1", "L1_gnn_W2", "L1_gnn_b2"]


def kernel(**inputs):
    import numpy as np
    import concourse.bacc as bacc
    from concourse import mybir as mb
    from concourse.bass_utils import run_bass_kernel_spmd

    nc = bacc.Bacc("TRN2", target_bir_lowering=False, num_devices=1)
    arrays, io = {}, {}
    for name in INS:
        a = np.ascontiguousarray(inputs[name])
        arrays[f"in_{name}"] = a
        io[name] = nc.dram_tensor(f"in_{name}", a.shape, mb.dt.from_np(a.dtype), kind="ExternalInput").ap()
    out = nc.dram_tensor("out_0", (N, D), mb.dt.float32, kind="ExternalOutput").ap()
    program(nc, io, out)
    r = run_bass_kernel_spmd(nc, [arrays], core_ids=[0])
    return r.results[0]["out_0"]
```

```python
from contextlib import ExitStack

import concourse.bass as bass
from concourse import mybir

P = 128
N = 12500
E = 200000
D = 64
D1 = D + 1
CH = 8
CE = CH * P
NCH = -(-E // CE)
FULL = E // CE
REST_P = (E - FULL * CE) // CH
HALF = NCH // 2
W = P
W_SHIFT = 7
WINDOWS = N // W + 1
ROWS = WINDOWS * W
LAST = N - (WINDOWS - 1) * W
GW = 7
GROUPS = WINDOWS // GW
UT = 8
UE = UT * P
UE_SHIFT = 10
UNITS = NCH * CE // UE + WINDOWS - 1
UNIT_COLS = -(-UNITS // P)
RING = 8
SHORT = RING // 2
PARTS = 3
EPS = 1e-5
assert GROUPS * GW == WINDOWS and HALF * 2 == NCH and NCH - FULL == 1 and REST_P * CH == E - FULL * CE
assert 1 << W_SHIFT == W and 1 << UE_SHIFT == UE

ALU = mybir.AluOpType
ACT = mybir.ActivationFunctionType
AX = mybir.AxisListType.X
F32 = mybir.dt.float32
BF16 = mybir.dt.bfloat16
I32 = mybir.dt.int32
U32 = mybir.dt.uint32


class Core:
    pass


class Own:

    def __init__(self, nc, own, name):
        self.nc, self.own, self.name, self.all = nc, own, name, []

    def tmp(self, s, shape, dt=F32):
        return self.own.enter_context(self.nc.sbuf_tensor(f"{self.name}_{s}", shape, dt))

    def psum(self, s, shape, dt=F32):
        return self.own.enter_context(self.nc.psum_tensor(f"{self.name}_{s}", shape, dt))

    def sem(self, s):
        self.all.append(self.own.enter_context(self.nc.semaphore(f"{self.name}_{s}")))
        return self.all[-1]

    def clear(self):
        for sem in self.all:
            self.nc.gpsimd.sem_clear(sem)

    def sems(self, *names):
        return [self.sem(s) for s in names]


def several(n, make, s, *a):
    return [make(f"{s}{h}", *a) for h in range(n)]


def pair(make, s, *a):
    return several(2, make, s, *a)


def wait_alone(eng, sem, value):
    if not isinstance(value, int):
        value = eng.to_reg(value)
    eng.wait_ge(sem, 1)
    eng.wait_ge(sem, value)


def link(eng, ins, sem, value):
    ins.then_inc(sem, 1)
    eng.wait_ge(sem, value)


MANY = 1 << 20


def in_rings(eng, count, ring, body, rounds=1):
    for s in range(ring * rounds):
        body(s, s % ring, s // ring, s)
    with eng.Fori(rounds, count // ring) as i:
        for r in range(ring):
            body(ring * i + r, r, i, MANY)
    for s in range(count // ring * ring, count):
        body(s, s % ring, s // ring, MANY)


def windows_of_rows(table):
    return table.rearrange("(w p) d -> p w d", p=P)


def wide(v, n, shape):
    return v.unsqueeze(n).to_broadcast(shape)


def norm_vector(dve, k, s, part_ready):
    n = WINDOWS // s.parts
    for i in range(s.parts):
        part = slice(i * n, (i + 1) * n)
        part_ready(i, part)
        link(dve, dve.tensor_reduce(s.sum[:, part], k.x[:, part, :], AX, ALU.add), s.step, i + 1)
        dve.scalar_tensor_tensor(k.centred[:, part, :], wide(s.sum[:, part], 2, [P, n, D]), -1.0 / D, k.x[:, part, :],
                                 ALU.mult, ALU.add).then_inc(s.centred, 1)
    for i in range(s.parts):
        part = slice(i * n, (i + 1) * n)
        dve.wait_ge(s.squared, i + 1)
        last = dve.tensor_reduce(s.var[:, part], s.square[:, part, :], AX, ALU.add)
    link(dve, last, s.step, s.parts + 1)
    dve.tensor_scalar(s.var[:], s.var[:], 1.0 / D, EPS, ALU.mult, ALU.add).then_inc(s.var_ready, 1)
    dve.wait_ge(s.root_ready, 1)
    link(dve, dve.reciprocal(s.rough[:], s.root[:]), s.step, s.parts + 2)
    link(dve, dve.tensor_tensor(s.fix[:], s.rough[:], s.rough[:], ALU.mult), s.step, s.parts + 3)
    link(dve, dve.tensor_tensor(s.fix[:], s.fix[:], s.var[:], ALU.mult), s.step, s.parts + 4)
    link(dve, dve.tensor_scalar(s.fix[:], s.fix[:], -0.5, 1.5, ALU.mult, ALU.add), s.step, s.parts + 5)
    dve.tensor_tensor(k.rstd[:], s.rough[:], s.fix[:], ALU.mult)


def norm_scalar(act, k, s):
    n = WINDOWS // s.parts
    for i in range(s.parts):
        act.wait_ge(s.centred, i + 1)
        act.activation(s.square[:, i * n:(i + 1) * n, :], k.centred[:, i * n:(i + 1) * n, :], ACT.Square).then_inc(s.squared, 1)
    act.wait_ge(s.var_ready, 1)
    act.activation(s.root[:], s.var[:], ACT.Sqrt).then_inc(s.root_ready, 1)


class Norm:

    def __init__(self, k, o):
        self.parts = 7
        self.square = k.own
        self.sum, self.var, self.root, self.rough, self.fix = (o.tmp(t, [P, WINDOWS]) for t in ("sum", "var", "root", "rough", "fix"))
        self.step, self.centred, self.squared, self.var_ready, self.root_ready = o.sems("step", "centred", "squared", "var_ready", "root_ready")


def constants(nc, ctx, k):
    def sb(name, shape, dt=F32):
        return ctx.enter_context(nc.sbuf_tensor(name, shape, dt))

    def dram(name, shape, dt=F32):
        return nc.dram_tensor(name, shape, dt).ap()

    k.ident = sb("ident", [P, P])
    k.ident_b = sb("ident_b", [P, P], BF16)
    k.before = sb("before", [P, P])
    k.ones = sb("ones", [P, P])
    k.before_b, k.ones_b = sb("before_b", [P, P], BF16), sb("ones_b", [P, P], BF16)
    k.iota = sb("iota", [P, W])
    k.window_neg = sb("window_neg", [P, WINDOWS])
    k.tile_before = sb("tile_before", [P, CH, CH])
    k.conv_w = [sb(f"conv{i}_w", [D, 2 * D]) for i in (1, 2)]
    k.conv_b = [sb(f"conv{i}_b", [P, D]) for i in (1, 2)]
    k.edge_ends = sb("edge_ends", [D, 2 * D])
    k.edge_attr_w = sb("edge_attr_w", [P, 2, D])
    k.edge_b1 = sb("edge_b1", [P, D])
    k.edge_out = sb("edge_out", [D1, D])
    k.src = sb("src_f", [P, NCH, CH])
    k.src_window = sb("src_window", [P, NCH, CH])
    k.dst_rel = sb("dst_rel", [P, NCH, CH])
    k.least_rel = sb("least_rel", [P, NCH])
    k.win_row = sb("win_row", [1, 4 * NCH], I32)
    k.x = sb("x", [P, WINDOWS, D])
    k.rstd = sb("rstd", [P, WINDOWS])
    k.acc = sb("acc", [P, WINDOWS + 1, D1])
    k.a_parts = sb("a_parts", [P, WINDOWS, PARTS, D], BF16)
    k.place = sb("place", [P, NCH, CH])
    k.inv_count = sb("inv_count", [P, WINDOWS])
    k.window_edges, k.next_place = sb("window_edges", [P, WINDOWS]), sb("next_place", [P, WINDOWS])
    k.step_row = sb("step_row", [1, 2 * UNIT_COLS * P], I32)
    k.step_node = sb("step_node", [P, UNITS])
    k.h_table, k.g_table = dram("h_table", [ROWS, PARTS * D], BF16), dram("g_table", [ROWS, PARTS * D], BF16)
    k.b_table = dram("b_table", [ROWS + W, PARTS * D], BF16)
    k.sorted = dram("sorted_edges", [NCH * CE, D1])
    k.windows = dram("windows", [5, NCH], I32)
    k.units = dram("units", [2, UNIT_COLS * P], I32)


def setup(nc, k, io):
    with ExitStack() as own:
        o = Own(nc, own, "setup")
        norm = Norm(k, Own(nc, own, "norm0"))
        ids = [o.tmp(f"{s}_ids", [HALF, 2, CE], I32) for s in ("src", "dst")]
        ids_f = [k.acc[0:HALF].rearrange("q w d -> q (w d)")[:, i * 2 * CE:(i + 1) * 2 * CE].rearrange("q (a e) -> q a e", a=2) for i in range(2)]
        zeros, w_rows = o.tmp("zeros", [P, PARTS * D], BF16), o.tmp("w_rows", [D, 4, D])
        least, most, first, last_w, count, span, rel = (o.tmp(s, [HALF, 2], I32) for s in ("least", "most", "first", "last_w", "count", "span", "rel"))
        first_f, least_f, most_f = (o.tmp(s, [HALF, 2]) for s in ("first_f", "least_f", "most_f"))
        rel_i, window_i = o.tmp("rel_i", [P, NCH], I32), o.tmp("window_i", [P, NCH, CH], I32)
        w_ps = o.psum("w_ps", [D, 8, D])
        ids_ps = pair(o.psum, "ids_ps", [P, 4, P])
        pieces = ((0,), (1, 2), (3, 4), (5, 6))
        x_landed = several(len(pieces), o.sem, "x_landed")
        ids_landed = [o.sem(f"{s}_landed") for s in ("src", "dst")]
        cleared, ids_cleared, x_cleared, masks, w_landed, ids_float, relative, ids_turned, ids_kept = o.sems(
            "cleared", "ids_cleared", "x_cleared", "masks", "w_landed", "ids_float", "relative", "ids_turned", "ids_kept")
        windows_made, windows_stored, rel_landed, row_landed, zeros_stored, w_turned, step = o.sems(
            "windows_made", "windows_stored", "rel_landed", "row_landed", "zeros_stored", "w_turned", "step")
        own.callback(o.clear)
        block = own.enter_context(nc.Block())

        @block.sync
        def _(sp):
            full = E // (2 * CE)
            rest = E - (2 * full + 1) * CE
            sp.wait_ge(ids_cleared, 1)
            for name, to, landed in (("dst", ids[1], ids_landed[1]), ("src", ids[0], ids_landed[0])):
                sp.dma_start(to[0:full], io[name][0:full * 2 * CE].rearrange("(q a e) -> q a e", a=2, e=CE)).then_inc(landed, 16)
                sp.dma_start(to[full:HALF, 0, :], io[name][full * 2 * CE:E - rest].rearrange("(a e) -> a e", a=1)).then_inc(landed, 16)
                sp.dma_start(to[full:HALF, 1, 0:rest], io[name][E - rest:E].rearrange("(a e) -> a e", a=1)).then_inc(landed, 16)
            sp.wait_ge(x_cleared, 1)
            n = WINDOWS // norm.parts
            x = windows_of_rows(io["x"][0:(WINDOWS - 1) * W, :])
            for i, piece in enumerate(pieces):
                part = slice(piece[0] * n, min((piece[-1] + 1) * n, WINDOWS - 1))
                sp.dma_start(k.x[:, part, :], x[:, part, :]).then_inc(x_landed[i], 16)
            sp.dma_start(k.x[0:LAST, WINDOWS - 1, :], io["x"][(WINDOWS - 1) * W:N, :]).then_inc(x_landed[-1], 16)
            sp.wait_ge(windows_made, 1)
            for i, w in enumerate((first, count, least, span, rel)):
                sp.dma_start(k.windows[i].rearrange("(q a) -> q a", a=2), w[:]).then_inc(windows_stored, 16)
            sp.wait_ge(windows_stored, 16 * 5)
            sp.dma_start(k.win_row[:], k.windows[0:4, :].rearrange("(o i) c -> o (i c)", o=1)).then_inc(row_landed, 16)
            sp.dma_start(rel_i[:], k.windows[4:5, :].to_broadcast([P, NCH])).then_inc(rel_landed, 16)
            sp.wait_ge(row_landed, 16)

        @block.scalar
        def _(act):
            for i, name in enumerate(("L0_gnn_W1l", "L0_gnn_W1r", "L0_gnn_W2l", "L0_gnn_W2r")):
                act.dma_start(w_rows[:, i, :], io[name]).then_inc(w_landed, 16)
            w1 = io["L1_gnn_W1"]
            for i in range(2):
                act.dma_start(k.edge_ends[:, (1 - i) * D:(2 - i) * D], w1[i * D:(i + 1) * D, :]).then_inc(w_landed, 16)
            for to, name in ((k.conv_b[0], "L0_gnn_b1"), (k.conv_b[1], "L0_gnn_b2"), (k.edge_b1, "L1_gnn_b1")):
                act.dma_start(to[:], io[name].rearrange("(a d) -> a d", a=1).to_broadcast([P, D])).then_inc(w_landed, 16)
            act.dma_start(k.edge_out[0:D, :], io["L1_gnn_W2"]).then_inc(w_landed, 16)
            act.dma_start(k.edge_out[D:D1, :], io["L1_gnn_b2"].rearrange("(a d) -> a d", a=1)).then_inc(w_landed, 16)
            act.wait_ge(cleared, 1)
            for i in range(2):
                act.dma_start(k.edge_attr_w[i * D:(i + 1) * D, i, :], w1[2 * D:3 * D, :]).then_inc(w_landed, 16)
            act.dma_start(k.b_table[ROWS:ROWS + W, :], zeros[:]).then_inc(zeros_stored, 16)
            for g in range(8):
                i, a, t = g // 4, g // 2 % 2, g % 2 * 4
                act.wait_ge(ids_turned, g + 1)
                to = (k.dst_rel, k.src)[i]
                act.copy(to[:].rearrange("p (q a) t -> p a t q", a=2)[:, a, t:t + 4, :], ids_ps[g % 2][:, :, 0:HALF]).then_inc(ids_kept, 1)
            norm_scalar(act, k, norm)
            act.wait_ge(zeros_stored, 16)
            act.wait_ge(w_landed, 16 * 13)

        @block.gpsimd
        def _(pool):
            pool.iota(k.iota[:], [[1, W]], base=0, channel_multiplier=0, allow_small_or_imprecise_dtypes=True)
            pool.iota(k.window_neg[:], [[-W, WINDOWS]], base=0, channel_multiplier=0, allow_small_or_imprecise_dtypes=True)
            pool.wait_ge(cleared, 1)
            pool.affine_select(out=k.ident[:], in_=k.ident[:], pattern=[[-1, P]], compare_op=ALU.not_equal, fill=1.0,
                               base=0, channel_multiplier=1).then_inc(masks, 1)
            pool.affine_select(out=k.before[:], in_=k.ones[:], pattern=[[1, P]], compare_op=ALU.is_gt, fill=0.0,
                               base=0, channel_multiplier=-1).then_inc(masks, 1)
            for i in (1, 0):
                pool.wait_ge(ids_landed[i], 48)
                pool.tensor_copy(ids_f[i][:], ids[i][:]).then_inc(ids_float, 1)

        @block.tensor
        def _(pe):
            pe.wait_ge(masks, 2)
            pe.wait_ge(w_landed, 16 * 13)
            for i in range(4):
                mm = pe.transpose(w_ps[:, i, :], w_rows[:, i, :], k.ident[0:D, 0:D])
            mm.then_inc(w_turned, 1)
            for g in range(8):
                i, a, t = g // 4, g // 2 % 2, g % 2 * 4
                if g == 0:
                    pe.wait_ge(relative, 2)
                if g == 4:
                    pe.wait_ge(ids_float, 2)
                if g >= 2:
                    pe.wait_ge(ids_kept, g - 1)
                for j in range(4):
                    mm = pe.transpose(ids_ps[g % 2][:, j, 0:HALF], ids_f[1 - i][:, a, :].rearrange("q (p t) -> q t p", t=CH)[:, t + j, :],
                                      k.ident[0:HALF, 0:HALF])
                mm.then_inc(ids_turned, 1)

        @block.vector
        def _(dve):
            for i in range(2):
                last = dve.memset(ids[i][96:HALF], N)
            last.then_inc(ids_cleared, 1)
            dve.memset(k.x[:, WINDOWS - 1, :], 0.0).then_inc(x_cleared, 1)
            dve.memset(zeros[:], 0.0)
            dve.memset(k.ident[:], 0.0)
            dve.memset(k.ones[:], 1.0)
            dve.memset(k.edge_attr_w[:], 0.0)
            link(dve, dve.memset(k.tile_before[:], 0.0), step, 1)
            for t in range(1, CH):
                dve.memset(k.tile_before[:, t, 0:t], 1.0)
            dve.sem_inc(cleared, 1)
            dve.wait_ge(ids_float, 1)
            dst = ids_f[1]
            dve.tensor_reduce(least_f[:], dst[:], AX, ALU.min)
            link(dve, dve.tensor_reduce(most_f[:], dst[:], AX, ALU.max), step, 2)
            dve.tensor_copy(least[:], least_f[:])
            link(dve, dve.tensor_copy(most[:], most_f[:]), step, 3)
            dve.tensor_scalar(first[:], least[:], W_SHIFT, None, ALU.arith_shift_right)
            dve.tensor_scalar(last_w[:], most[:], W_SHIFT, None, ALU.arith_shift_right)
            link(dve, dve.tensor_tensor(span[:], most[:], least[:], ALU.subtract), step, 4)
            dve.tensor_tensor(count[:], last_w[:], first[:], ALU.subtract)
            dve.tensor_scalar(span[:], span[:], W_SHIFT, None, ALU.arith_shift_right)
            link(dve, dve.tensor_scalar(first_f[:], first[:], W, None, ALU.mult), step, 5)
            dve.tensor_scalar(count[:], count[:], 1, None, ALU.add)
            dve.tensor_scalar(span[:], span[:], 1, None, ALU.add)
            dve.tensor_tensor(rel[:], least_f[:], first_f[:], ALU.subtract).then_inc(windows_made, 1)
            for a in range(2):
                dve.tensor_scalar(dst[:, a, :], dst[:, a, :], first_f[:, a:a + 1], None, ALU.subtract).then_inc(relative, 1)
            dve.wait_ge(w_turned, 1)
            for i in range(2):
                dve.tensor_copy(k.conv_w[i][:], w_ps[:, 2 * i:2 * i + 2, :].rearrange("i s o -> i (s o)"))
            for to, mask in ((k.ident_b, k.ident), (k.before_b, k.before), (k.ones_b, k.ones)):
                dve.tensor_copy(to[:], mask[:])

            def part_ready(i, part):
                for j, piece in enumerate(pieces):
                    if i == piece[0]:
                        dve.wait_ge(x_landed[j], 32 if j == len(pieces) - 1 else 16)

            norm_vector(dve, k, norm, part_ready)
            dve.wait_ge(ids_kept, 8)
            link(dve, dve.tensor_copy(window_i[:], k.src[:]), step, 6)
            link(dve, dve.tensor_scalar(window_i[:], window_i[:], W_SHIFT, None, ALU.arith_shift_right), step, 7)
            dve.tensor_copy(k.src_window[:], window_i[:])
            dve.wait_ge(rel_landed, 16)
            dve.tensor_copy(k.least_rel[:], rel_i[:])


def project(nc, k, name, depth, weights, feed, relu, table, keep, steps=False, out=None):
    with ExitStack() as own:
        o = Own(nc, own, name)
        cols = weights.shape[-1]
        stage, h_t = pair(o.tmp, "stage", [P, GW, depth]), pair(o.tmp, "h_t", [depth, GW, P])
        rows = pair(o.tmp, "rows", [P, GW, D]) if table is None else pair(o.tmp, "rows", [P, GW, PARTS, D], BF16)
        left = pair(o.tmp, "left", [P, GW, D]) if table is not None else (None, None)
        turn_ps, rows_ps = pair(o.psum, "turn_ps", [P, GW + 1, P]), pair(o.psum, "rows_ps", [P, GW + 1, P])
        staged, turned, h_t_ready, product, kept = o.sems("staged", "turned", "h_t_ready", "product", "kept")
        first_ready, second_ready, rows_ready = o.sems("first_ready", "second_ready", "rows_ready") if table is not None else (None, None, None)
        step = o.sem("step") if steps else None
        stored = pair(o.sem, "stored")
        block = own.enter_context(nc.Block())
        last = GROUPS - 1

        def staggered(eng, *stages):
            def body(g, h, used, n):
                for stage, lag in stages:
                    if n >= lag:
                        stage(g - lag, (h - lag) % 2, used + (h - lag) // 2, n if n == MANY else n - lag)

            in_rings(eng, GROUPS, 2, body, rounds=2)
            for late in range(1, 1 + max(lag for _, lag in stages)):
                for stage, lag in stages:
                    if lag >= late:
                        g = last + late - lag
                        stage(g, g % 2, g // 2, MANY)

        @block.vector
        def _(dve):
            def put(g, h, used, n):
                if n >= 2:
                    dve.wait_ge(turned, g - 1)
                feed(dve, stage[h], g, step).then_inc(staged, 1)

            def take(g, h, used, n):
                if table is None:
                    dve.wait_ge(product, g + 1)
                    if n >= 2:
                        dve.wait_ge(stored[h], 16 * used)
                    keep(dve, rows_ps[h][:, 0:GW, 0:cols], g, rows[h], step).then_inc(kept, 1)
                    return
                dve.wait_ge(first_ready, g + 1)
                dve.tensor_tensor(left[h][:], rows_ps[h][:, 0:GW, 0:D], rows[h][:, :, 0, :], ALU.subtract)
                keep(dve, rows_ps[h][:, 0:GW, D:cols], g, None, step).then_inc(kept, 1)

            def third_part(g, h, used, n):
                dve.wait_ge(second_ready, g + 1)
                dve.tensor_tensor(rows[h][:, :, 2, :], left[h][:], rows[h][:, :, 1, :], ALU.subtract).then_inc(rows_ready, 1)

            if table is None:
                staggered(dve, (put, 0), (take, 2))
            else:
                staggered(dve, (put, 0), (third_part, 3), (take, 2))

        @block.tensor
        def _(pe):
            def turn(g, h, used, n):
                wait_alone(pe, staged, g + 1)
                if n >= 2:
                    wait_alone(pe, h_t_ready, g - 1)
                for i in range(GW):
                    mm = pe.transpose(turn_ps[h][0:depth, i, :], stage[h][:, i, :], k.ident[:])
                mm.then_inc(turned, 1)

            def products(g, h, used, n):
                pe.wait_ge(h_t_ready, g + 1)
                if n >= 2:
                    pe.wait_ge(kept, g - 1)
                for i in range(GW):
                    mm = pe.matmul(rows_ps[h][:, i, 0:cols], h_t[h][:, i, :], weights[:], start=True, stop=True)
                mm.then_inc(product, 1)

            staggered(pe, (turn, 1), (products, 2))

        @block.scalar
        def _(act):
            def turn_back(g, h, used, n):
                act.wait_ge(turned, g + 1)
                if n >= 2:
                    act.wait_ge(product, g - 1)
                act.activation(h_t[h][:], turn_ps[h][0:depth, 0:GW, :], ACT.Relu if relu else ACT.Copy).then_inc(h_t_ready, 1)

            def first_part(g, h, used, n):
                act.wait_ge(product, g + 1)
                if n >= 2:
                    act.wait_ge(stored[h], 16 * used)
                act.copy(rows[h][:, :, 0, :], rows_ps[h][:, 0:GW, 0:D]).then_inc(first_ready, 1)

            def second_part(g, h, used, n):
                act.wait_ge(kept, g + 1)
                act.copy(rows[h][:, :, 1, :], left[h][:]).then_inc(second_ready, 1)

            if table is None:
                staggered(act, (turn_back, 1))
            else:
                staggered(act, (turn_back, 1), (second_part, 3), (first_part, 2))

        @block.sync
        def _(sp):
            to = windows_of_rows(out[0:(WINDOWS - 1) * W, :] if out is not None else table[0:ROWS, :])

            def body(g, h, used, n):
                sp.wait_ge(kept if table is None else rows_ready, g + 1)
                if out is not None and isinstance(g, int) and g == last:
                    sp.dma_start(to[:, g * GW:WINDOWS - 1, :], rows[h][:, 0:GW - 1, :]).then_inc(stored[h], 16)
                    sp.dma_start(out[(WINDOWS - 1) * W:N, :], rows[h][0:LAST, GW - 1, :]).then_inc(stored[h], 16)
                else:
                    sp.dma_start(to[:, bass.ds(g * GW, GW), :], rows[h][:] if table is None else rows[h][:].rearrange("p w i d -> p w (i d)")).then_inc(stored[h], 16)

            for g in range(2):
                body(g, g, 0, g)
            with sp.Fori(1, GROUPS // 2 - 1) as i:
                for h in range(2):
                    body(2 * i + h, h, i, MANY)
            for g in (last - 1, last):
                body(g, g % 2, g // 2, MANY)
            for h in range(2):
                sp.wait_ge(stored[h], 16 * (GROUPS // 2) + (16 if out is not None and h == last % 2 else 0))


def sum_by_dst(nc, k, name, table, acc, before_edges, sorting):
    with ExitStack() as own:
        o = Own(nc, own, name)
        rows, one_hot = o.tmp("rows", [P, 2, CH, PARTS * D + 1], BF16), o.tmp("one_hot", [P, 2, 2, CH, W], BF16)
        index, shifted = pair(o.tmp, "index", [P, CH], U32), o.tmp("shifted", [P, CH])
        more_hot = o.tmp("more_hot", [P, CH, W], BF16)
        s = sorting(k, o)
        iota = o.psum("iota", [P, 512])
        sums, more_sums = pair(o.psum, "sums", [P, 4, P]), o.psum("more_sums", [P, 512])
        index_ready, landed, rows_used = (pair(o.sem, t) for t in ("index_ready", "landed", "rows_used"))
        begun, hot_ready, product, added, shift_done, more_ready, more_product, more_added, more_shifted = o.sems(
            "begun", "hot_ready", "product", "added", "shift_done", "more_ready", "more_product", "more_added", "more_shifted")
        block = own.enter_context(nc.Block())

        @block.gpsimd
        def _(pool):
            pool.wait_ge(begun, 1)
            with pool.Fori(0, NCH // 2) as i:
                for h in range(2):
                    wait_alone(pool, index_ready[h], i + 1)
                    for t in range(CH):
                        pool.indirect_dma_start(rows[:, h, t, 0:PARTS * D], None, table,
                                                bass.IndirectOffsetOnAxis(ap=index[h][:, t:t + 1], axis=0)).then_inc(landed[h], 16)

        @block.scalar
        def _(act):
            def put_index(c, h):
                act.copy(index[h][:], k.src[:, bass.ds(c, 1), :].rearrange("p c t -> p (c t)")).then_inc(index_ready[h], 1)

            for h in range(2):
                put_index(h, h)
            with act.Fori(1, NCH // 2) as i:
                for h in range(2):
                    act.wait_ge(rows_used[h], i)
                    put_index(2 * i + h, h)

        @block.tensor
        def _(pe):
            windows = pe.alloc_register(f"{name}_pe_windows")
            pe.reg_mov(windows, 0)

            def add_up(to, hot, h):
                for i in (2, 0, 1):
                    n = D1 if i == 2 else D
                    for t in range(CH):
                        mm = pe.matmul(to[:, 0:n], hot[:, t, :], rows[:, h, t, i * D:i * D + n], start=(i == 2 and t == 0), stop=(i == 1 and t == CH - 1), skip_group_check=True)
                return mm

            def chunk(c, h, used, first):
                count = pe.value_load(k.win_row[0:1, bass.ds(NCH + c, 1)], min_val=1, max_val=WINDOWS)
                s.prefix(pe, c, h)
                wait_alone(pe, landed[h], 16 * CH * (used + 1))
                pe.wait_ge(hot_ready, c + 1)
                if not first:
                    pe.wait_ge(added, c - 1)
                for w in range(2):
                    mm = add_up(sums[h][:, w, :], one_hot[:, h, w], h)
                mm.then_inc(product, 1)
                with pe.If(count > 2):
                    with pe.Fori(2, count):
                        pe.reg_add(windows, windows, 1)
                        pe.wait_ge(more_ready, pe.snap(windows, min_val=1, max_val=NCH * WINDOWS))
                        add_up(more_sums, more_hot, h).then_inc(more_product, 1)

            for h in range(2):
                chunk(h, h, 0, True)
            with pe.Fori(1, NCH // 2) as i:
                for h in range(2):
                    chunk(2 * i + h, h, i, False)

        @block.vector
        def _(dve):
            dve.memset(rows[:], 1.0).then_inc(begun, 1)
            dve.tensor_copy(iota[:, 0:W], k.iota[:]).then_inc(begun, 1)
            link(dve, dve.memset(acc[:], 0.0), begun, 3)
            before_edges(dve)
            s.clear(dve)
            windows, first = dve.alloc_register(f"{name}_dve_windows"), dve.alloc_register(f"{name}_dve_first")
            dve.reg_mov(windows, 0)
            shape = [P, CH, W]

            def make_hot(to, rel):
                return dve.tensor_tensor(to, wide(iota[:, 0:W], 1, shape), wide(rel, 2, shape), ALU.is_equal)

            def shift(rel, w):
                return dve.tensor_scalar(shifted[:], rel, k.window_neg[:, bass.ds(w, 1)], None, ALU.add)

            def node_rows(at, n):
                return acc[:, bass.ds(at, n), :]

            def make(c, h):
                rel = k.dst_rel[:, bass.ds(c, 1), :].rearrange("p c t -> p (c t)")
                if not (isinstance(c, int) and c == 0):
                    dve.wait_ge(hot_ready, c)
                link(dve, shift(rel, 1), shift_done, c + 1)
                make_hot(one_hot[:, h, 0], rel)
                make_hot(one_hot[:, h, 1], shifted[:]).then_inc(hot_ready, 1)

            def windows_of(c):
                count = dve.value_load(k.win_row[0:1, bass.ds(c + NCH, 1)], min_val=1, max_val=WINDOWS)
                return count, dve.value_load(k.win_row[0:1, bass.ds(c, 1)], min_val=0, max_val=WINDOWS - 1)

            def add(c, h, count, base):
                part = node_rows(base, 2)
                dve.wait_ge(product, c + 1)
                if not (isinstance(c, int) and c == 0):
                    dve.wait_ge(added, c)
                dve.tensor_tensor(part, part, sums[h][:, 0:2, 0:D1], ALU.add).then_inc(added, 1)
                dve.reg_mov(first, base)
                with dve.If(count > 2):
                    with dve.Fori(2, count) as w:
                        dve.reg_add(windows, windows, 1)
                        number = dve.snap(windows, min_val=1, max_val=NCH * WINDOWS)
                        more = node_rows(dve.snap(first, min_val=0, max_val=WINDOWS - 3) + 2, 1).rearrange("p w d -> p (w d)")
                        dve.wait_ge(hot_ready, c + 1 if isinstance(c, int) and c == NCH - 1 else c + 2)
                        dve.wait_ge(added, c + 1)
                        link(dve, shift(k.dst_rel[:, bass.ds(c, 1), :].rearrange("p c t -> p (c t)"), w), more_shifted, number)
                        make_hot(more_hot[:], shifted[:]).then_inc(more_ready, 1)
                        dve.wait_ge(more_product, number)
                        link(dve, dve.tensor_tensor(more, more, more_sums[:, 0:D1], ALU.add), more_added, number)
                        dve.reg_add(first, first, 1)
                dve.sem_inc(rows_used[h], 1)

            def both(c, h):
                make(c, h)
                count, base = windows_of(c - 1)
                s.members(dve, c, h)
                add(c - 1, 1 - h, count, base)
                s.sort(dve, c, h)

            make(0, 0)
            s.members(dve, 0, 0)
            s.sort(dve, 0, 0)
            with dve.Fori(0, NCH // 2 - 1) as i:
                both(2 * i + 1, 1)
                both(2 * i + 2, 0)
            both(NCH - 1, 1)
            add(NCH - 1, 1, *windows_of(NCH - 1))


class Counting:

    def __init__(self, k, o):
        self.k, self.member, self.edges = k, o.tmp("member", [P, WINDOWS, CH]), o.tmp("edges", [P, WINDOWS])
        self.same = o.tmp("same", [P, CH, CH])
        self.step = o.sem("sort_step")

    def prefix(self, pe, c, h):
        pass

    def clear(self, dve):
        link(dve, dve.memset(self.k.window_edges[:], 0.0), self.step, 1)

    def members(self, dve, c, h):
        shape = [P, WINDOWS, CH]
        link(dve, dve.tensor_tensor(self.member[:], wide(self.k.iota[:, 0:WINDOWS], 2, shape),
                                    self.k.src_window[:, bass.ds(c, 1), :].to_broadcast(shape), ALU.is_equal), self.step, 5 * c + 2)
        dve.tensor_reduce(self.edges[:], self.member[:], AX, ALU.add).then_inc(self.step, 1)

    def sort(self, dve, c, h):
        k, shape = self.k, [P, CH, CH]
        window = k.src_window[:, bass.ds(c, 1), :].rearrange("p c t -> p (c t)")
        link(dve, dve.tensor_tensor(self.same[:], wide(window, 2, shape), wide(window, 1, shape), ALU.is_equal), self.step, 5 * c + 4)
        dve.tensor_tensor(k.window_edges[:], k.window_edges[:], self.edges[:], ALU.add)
        link(dve, dve.tensor_tensor(self.same[:], self.same[:], k.tile_before[:], ALU.mult), self.step, 5 * c + 5)
        link(dve, dve.tensor_reduce(k.place[:, bass.ds(c, 1), :].rearrange("p c t -> p (c t)"), self.same[:], AX, ALU.add), self.step, 5 * c + 6)


class Ranking:

    def __init__(self, k, o):
        self.k, self.member = k, pair(o.tmp, "member", [P, CH, WINDOWS], BF16)
        self.places, self.chosen, self.first = o.tmp("places", [P, WINDOWS]), o.tmp("chosen", [P, CH, WINDOWS]), o.tmp("first", [P, CH])
        self.before_ps = o.psum("before_ps", [P, 4, P])
        self.members_ready, self.before_ready, self.step = o.sems("members_ready", "before_ready", "sort_step")

    def prefix(self, pe, c, h):
        pe.wait_ge(self.members_ready, c + 1)
        for i, mask in enumerate((self.k.before_b, self.k.ones_b)):
            for t in range(CH):
                mm = pe.matmul(self.before_ps[:, i, 0:WINDOWS], mask[:], self.member[h][:, t, :], start=(t == 0), stop=(t == CH - 1))
        mm.then_inc(self.before_ready, 1)

    def clear(self, dve):
        pass

    def members(self, dve, c, h):
        shape = [P, CH, WINDOWS]
        dve.tensor_tensor(self.member[h][:], wide(self.k.iota[:, 0:WINDOWS], 1, shape),
                          wide(self.k.src_window[:, bass.ds(c, 1), :].rearrange("p c t -> p (c t)"), 2, shape), ALU.is_equal).then_inc(self.members_ready, 1)

    def sort(self, dve, c, h):
        k = self.k
        dve.wait_ge(self.before_ready, c + 1)
        link(dve, dve.tensor_tensor(self.places[:], self.before_ps[:, 0, 0:WINDOWS], k.next_place[:], ALU.add), self.step, 5 * c + 1)
        link(dve, dve.tensor_tensor(self.chosen[:], self.member[h][:], wide(self.places[:], 1, [P, CH, WINDOWS]), ALU.mult), self.step, 5 * c + 2)
        dve.tensor_tensor(k.next_place[:], self.before_ps[:, 1, 0:WINDOWS], k.next_place[:], ALU.add).then_inc(self.step, 1)
        link(dve, dve.tensor_reduce(self.first[:], self.chosen[:], AX, ALU.add), self.step, 5 * c + 4)
        place = k.place[:, bass.ds(c, 1), :].rearrange("p c t -> p (c t)")
        link(dve, dve.tensor_tensor(place, place, self.first[:], ALU.add), self.step, 5 * c + 5)


def plan_units(nc, k):
    with ExitStack() as own:
        o = Own(nc, own, "plan")
        total, totals, start_f, own_step = o.tmp("total", [WINDOWS, 1]), o.tmp("totals", [WINDOWS, P]), o.tmp("start_f", [P, WINDOWS]), o.tmp("own_step", [P, WINDOWS])
        start_i, step_no = o.tmp("start_i", [P, WINDOWS], I32), o.tmp("step_no", [P, UNIT_COLS])
        not_past = o.tmp("not_past", [P, UNIT_COLS, WINDOWS - 1])
        window, window_i, unit_i = o.tmp("window", [P, UNIT_COLS]), o.tmp("window_i", [P, UNIT_COLS], I32), o.tmp("unit_i", [P, UNIT_COLS], I32)
        window_all = o.tmp("window_all", [P, UNIT_COLS * P], I32)
        ps = o.psum("ps", [P, 2, P])
        summed, total_ready, started, steps_made, made, stored, landed, numbered = o.sems(
            "summed", "total_ready", "started", "steps_made", "made", "stored", "landed", "numbered")
        block = own.enter_context(nc.Block())

        @block.gpsimd
        def _(pool):
            pool.iota(step_no[:], [[1, UNIT_COLS]], base=0, channel_multiplier=UNIT_COLS, allow_small_or_imprecise_dtypes=True).then_inc(numbered, 1)

        @block.tensor
        def _(pe):
            pe.matmul(ps[0:WINDOWS, 0, 0:1], k.window_edges[:], k.ones[:, 0:1], start=True, stop=True).then_inc(summed, 1)
            pe.wait_ge(total_ready, 1)
            pe.matmul(ps[:, 1, 0:WINDOWS], totals[:], k.before[0:WINDOWS, 0:WINDOWS], start=True, stop=True).then_inc(started, 1)

        @block.vector
        def _(dve):
            dve.wait_ge(summed, 1)
            link(dve, dve.tensor_copy(total[:], ps[0:WINDOWS, 0, 0:1]), made, 1)
            dve.tensor_scalar(totals[:], k.ones[0:WINDOWS, :], total[:, 0:1], None, ALU.mult).then_inc(total_ready, 1)
            dve.wait_ge(started, 1)
            dve.tensor_copy(k.next_place[:], ps[:, 1, 0:WINDOWS])
            link(dve, dve.tensor_copy(start_i[:], ps[:, 1, 0:WINDOWS]), made, 2)
            link(dve, dve.tensor_scalar(start_i[:], start_i[:], UE_SHIFT, None, ALU.arith_shift_right), made, 3)
            link(dve, dve.tensor_copy(start_f[:], start_i[:]), made, 4)
            link(dve, dve.tensor_tensor(own_step[:], start_f[:], k.iota[:, 0:WINDOWS], ALU.add), made, 5)
            dve.wait_ge(numbered, 1)
            shape = [P, UNIT_COLS, WINDOWS - 1]
            link(dve, dve.tensor_tensor(not_past[:], wide(own_step[:, 1:WINDOWS], 1, shape), wide(step_no[:], 2, shape), ALU.is_le), made, 6)
            link(dve, dve.tensor_reduce(window[:], not_past[:], AX, ALU.add), made, 7)
            dve.tensor_copy(window_i[:], window[:])
            dve.tensor_tensor(unit_i[:], step_no[:], window[:], ALU.subtract).then_inc(steps_made, 1)
            inverse_counts(dve, k, made, 8)
            dve.wait_ge(landed, 32)
            dve.tensor_scalar(k.step_node[:], window_all[:, 0:UNITS], W, None, ALU.mult)

        @block.sync
        def _(sp):
            sp.wait_ge(steps_made, 1)
            for i, v in enumerate((window_i, unit_i)):
                sp.dma_start(k.units[i].rearrange("(p a) -> p a", p=P), v[:]).then_inc(stored, 16)
            sp.wait_ge(stored, 32)
            sp.dma_start(k.step_row[:], k.units.rearrange("(o i) u -> o (i u)", o=1)).then_inc(landed, 16)
            sp.dma_start(window_all[:], k.units[0:1, :].to_broadcast([P, UNIT_COLS * P])).then_inc(landed, 16)
            sp.wait_ge(landed, 32)


def second_norm(nc, k, acc):
    with ExitStack() as own:
        o = Own(nc, own, "norm1")
        norm, mean_ready, x_ready = Norm(k, o), o.sem("mean_ready"), o.sem("x_ready")
        block = own.enter_context(nc.Block())

        @block.vector
        def _(dve):
            def part_ready(i, part):
                n = WINDOWS // norm.parts
                mean = norm.square
                link(dve, dve.tensor_tensor(mean[:, part, :], acc[:, part, 0:D], wide(k.inv_count[:, part], 2, [P, n, D]), ALU.mult), mean_ready, i + 1)
                link(dve, dve.tensor_tensor(k.x[:, part, :], k.x[:, part, :], mean[:, part, :], ALU.add), x_ready, i + 1)

            norm_vector(dve, k, norm, part_ready)

        @block.scalar
        def _(act):
            norm_scalar(act, k, norm)


def place_edges(nc, k, edge_attr):
    with ExitStack() as own:
        o = Own(nc, own, "place")
        attr, b_win, index = pair(o.tmp, "attr", [P, CH * D]), pair(o.tmp, "b_win", [W, PARTS * D], BF16), pair(o.tmp, "index", [P, CH], U32)
        more_rows, further_hot = o.tmp("more_rows", [W, PARTS * D], BF16), o.tmp("further_hot", [P, CH, W], BF16)
        hot, hot_t, rows = pair(o.tmp, "hot", [P, CH, W], BF16), pair(o.tmp, "hot_t", [W, CH, P], BF16), pair(o.tmp, "rows", [P, CH, D1])
        attr_t, rel, shifted = pair(o.tmp, "attr_t", [P, CH // 2, P]), pair(o.tmp, "rel", [P, CH]), o.tmp("shifted", [P, CH])
        left = pair(o.tmp, "left", [P, D])
        iota, rows_ps = o.psum("iota", [P, 512]), pair(o.psum, "rows_ps", [P, CH, D])
        attr_ps, hot_ps = pair(o.psum, "attr_ps", [P, CH // 2, P]), pair(o.psum, "hot_ps", [P, CH, P], BF16)
        loaded, b_landed, scattered = (pair(o.sem, s) for s in ("loaded", "b_landed", "scattered"))
        cleared, iota_set, rel_ready, hot_ready, turned, attr_ready, hot_t_ready, first_done, product = o.sems(
            "cleared", "iota_set", "rel_ready", "hot_ready", "turned", "attr_ready", "hot_t_ready", "first_done", "product")
        more_landed, more_shifted, more_hot, more_turned, more_ready, more_done = o.sems(
            "more_landed", "more_shifted", "more_hot", "more_turned", "more_ready", "more_done")
        rows_ready, src_ready, index_ready, split = o.sems("rows_ready", "src_ready", "index_ready", "split")
        block = own.enter_context(nc.Block())

        def in_turn(eng, ahead, rest):
            def both(c, h, used, n):
                ahead(c, h, used, n)
                if n >= 1:
                    rest(c - 1, 1 - h, used - 1 + h, n - 1)

            for c in range(2):
                both(c, c, 0, c)
            with eng.Fori(1, NCH // 2 - 1) as i:
                for h in range(2):
                    both(2 * i + h, h, i, MANY)
            for c in (NCH - 2, NCH - 1):
                both(c, c % 2, c // 2, MANY)
            rest(NCH - 1, 1, NCH // 2 - 1, MANY)

        def further_windows(eng, c, body):
            count = eng.value_load(k.win_row[0:1, bass.ds(c + 3 * NCH, 1)], min_val=1, max_val=WINDOWS)
            with eng.If(count > 1):
                with eng.Fori(1, count) as w:
                    eng.reg_add(number[eng], number[eng], 1)
                    body(w, eng.snap(number[eng], min_val=1, max_val=NCH * WINDOWS))

        number = {}

        def count_further(eng, s):
            number[eng] = eng.alloc_register(f"place_{s}_further")
            eng.reg_mov(number[eng], 0)

        @block.sync
        def _(sp):
            count_further(sp, "sp")
            at = sp.alloc_register("place_sp_at")
            sp.wait_ge(cleared, 1)

            def least_of(c):
                return sp.value_load(k.win_row[0:1, bass.ds(c + 2 * NCH, 1)], min_val=0, max_val=N)

            def load(c, h, used, n):
                least = least_of(c)
                if n >= 2:
                    sp.wait_ge(turned, c - 1)
                if isinstance(c, int) and c == NCH - 1:
                    sp.dma_start(attr[h][0:REST_P, :], edge_attr[FULL * CE:E, :].rearrange("(p t) d -> p (t d)", t=CH)).then_inc(loaded[h], 16)
                else:
                    sp.dma_start(attr[h][:], edge_attr.rearrange("(p t) d -> p (t d)", t=CH)[bass.ds(c * P, P), :]).then_inc(loaded[h], 16)
                if n >= 2:
                    sp.wait_ge(first_done, c - 1)
                sp.dma_start(b_win[h][:], k.b_table[bass.ds(least, W), :]).then_inc(b_landed[h], 16)

            def further(c, h, used, n):
                sp.reg_mov(at, least_of(c))

                def window(w, number):
                    sp.wait_ge(more_hot, number)
                    sp.reg_add(at, at, W)
                    sp.dma_start(more_rows[:], k.b_table[bass.ds(sp.snap(at, min_val=0, max_val=N), W), :]).then_inc(more_landed, 16)

                further_windows(sp, c, window)

            in_turn(sp, load, further)

        @block.gpsimd
        def _(pool):
            def ahead(c, h, used, n):
                wait_alone(pool, rows_ready, c + 1)
                wait_alone(pool, src_ready, c + 1)
                wait_alone(pool, index_ready, c + 1)
                for t in range(CH):
                    pool.indirect_dma_start(k.sorted, bass.IndirectOffsetOnAxis(ap=index[h][:, t:t + 1], axis=0), rows[h][:, t, :], None).then_inc(scattered[h], 16)

            in_turn(pool, ahead, lambda c, h, used, n: None)
            for h in range(2):
                pool.wait_ge(scattered[h], 16 * CH * (NCH // 2))

        @block.tensor
        def _(pe):
            count_further(pe, "pe")

            def turn_hot(h, one_hot):
                for t in range(CH):
                    mm = pe.transpose(hot_ps[h][:, t, :], one_hot[:, t, :], k.ident_b[:])
                return mm

            def add_b(h, b):
                for t in range(CH):
                    for i in range(PARTS):
                        mm = pe.matmul(rows_ps[h][:, t, :], hot_t[h][:, t, :], b[:, i * D:(i + 1) * D], start=False,
                                       stop=(t == CH - 1 and i == PARTS - 1), skip_group_check=True)
                return mm

            def turn(c, h, used, n):
                wait_alone(pe, loaded[h], 16 * (used + 1))
                wait_alone(pe, hot_ready, c + 1)
                if n >= 2:
                    wait_alone(pe, hot_t_ready, c - 1)
                for j in range(CH // 2):
                    pe.transpose(attr_ps[h][:, j, :], attr[h][:, j * P:(j + 1) * P], k.ident[:])
                turn_hot(h, hot[h]).then_inc(turned, 1)

            def products(c, h, used, n):
                pe.wait_ge(attr_ready, c + 1)
                if n >= 2:
                    pe.wait_ge(rows_ready, c - 1)
                for t in range(CH):
                    pe.matmul(rows_ps[h][:, t, :], attr_t[h][:, t // 2, :], k.edge_attr_w[:, t % 2, :], start=(t == 0), stop=False, skip_group_check=True)
                pe.wait_ge(hot_t_ready, c + 1)
                wait_alone(pe, b_landed[h], 16 * (used + 1))
                add_b(h, b_win[h]).then_inc(first_done, 1)

                def window(w, number):
                    wait_alone(pe, more_hot, number)
                    turn_hot(h, further_hot).then_inc(more_turned, 1)
                    pe.wait_ge(more_ready, number)
                    wait_alone(pe, more_landed, number * 16)
                    add_b(h, more_rows).then_inc(more_done, 1)

                further_windows(pe, c, window)
                pe.wait_ge(first_done, c + 1)
                pe.wait_ge(more_done, pe.snap(number[pe], min_val=0, max_val=NCH * WINDOWS) + 1)
                pe.sem_inc(product, 1)

            in_turn(pe, turn, products)

        @block.scalar
        def _(act):
            count_further(act, "act")

            def turned_back(c, h, used, n):
                act.wait_ge(turned, c + 1)
                if n >= 2:
                    act.wait_ge(product, c - 1)
                act.copy(attr_t[h][:], attr_ps[h][:]).then_inc(attr_ready, 1)
                act.copy(hot_t[h][:], hot_ps[h][:]).then_inc(hot_t_ready, 1)

            def rest(c, h, used, n):
                def window(w, number):
                    act.wait_ge(more_turned, number)
                    act.copy(hot_t[h][:], hot_ps[h][:]).then_inc(more_ready, 1)

                further_windows(act, c, window)
                act.wait_ge(product, c + 1)
                if n >= 2:
                    act.wait_ge(scattered[h], 16 * CH * used)
                act.copy(index[h][:], k.place[:, bass.ds(c, 1), :].rearrange("p c t -> p (c t)")).then_inc(index_ready, 1)
                act.copy(rows[h][:, :, 0:D], rows_ps[h][:]).then_inc(rows_ready, 1)

            in_turn(act, turned_back, rest)

        @block.vector
        def _(dve):
            count_further(dve, "dve")
            dve.memset(attr[1][:], 0.0).then_inc(cleared, 1)
            link(dve, dve.tensor_copy(iota[:, 0:W], k.iota[:]), iota_set, 1)
            dve.sem_inc(more_done, 1)
            shape = [P, CH, W]

            def make_hot(to, offset):
                return dve.tensor_tensor(to[:], wide(iota[:, 0:W], 1, shape), wide(offset[:], 2, shape), ALU.is_equal)

            def split_window(w):
                def part(i):
                    return k.a_parts[:, bass.ds(w, 1), i, :].rearrange("p w d -> p (w d)")

                a = k.own[:, bass.ds(w, 1), :].rearrange("p w d -> p (w d)")
                link(dve, dve.tensor_copy(part(0), a), split, 4 * w + 1)
                link(dve, dve.tensor_tensor(left[0][:], a, part(0), ALU.subtract), split, 4 * w + 2)
                link(dve, dve.tensor_copy(part(1), left[0][:]), split, 4 * w + 3)
                link(dve, dve.tensor_tensor(part(2), left[0][:], part(1), ALU.subtract), split, 4 * w + 4)

            def ahead(c, h, used, n):
                if n >= 2:
                    dve.wait_ge(turned, c - 1)
                link(dve, dve.tensor_scalar(rel[h][:], k.dst_rel[:, bass.ds(c, 1), :].rearrange("p c t -> p (c t)"), k.least_rel[:, bass.ds(c, 1)], None, ALU.subtract),
                     rel_ready, c + 1)
                make_hot(hot[h], rel[h]).then_inc(hot_ready, 1)
                if h == 0:
                    split_window(used)

            def rest(c, h, used, n):
                def window(w, number):
                    dve.wait_ge(first_done, c + 1)
                    dve.wait_ge(more_done, number)
                    link(dve, dve.tensor_scalar(shifted[:], rel[h][:], k.window_neg[:, bass.ds(w, 1)], None, ALU.add), more_shifted, number)
                    make_hot(further_hot, shifted).then_inc(more_hot, 1)

                further_windows(dve, c, window)
                if n >= 2:
                    dve.wait_ge(scattered[h], 16 * CH * used)
                dve.tensor_copy(rows[h][:, :, D], k.src[:, bass.ds(c, 1), :].rearrange("p c t -> p (c t)")).then_inc(src_ready, 1)

            in_turn(dve, ahead, rest)


def sum_by_src(nc, k, acc):
    with ExitStack() as own:
        o = Own(nc, own, "by_src")
        edges, rel = several(RING, o.tmp, "edges", [P, UT * D1]), several(SHORT, o.tmp, "rel", [P, UT])
        hot, hot_t = several(RING, o.tmp, "hot", [P, UT, W], BF16), pair(o.tmp, "hot_t", [W, UT, P], BF16)
        total, left = (several(SHORT, o.tmp, s, [P, UT, D]) for s in ("total", "left"))
        parts = several(RING, o.tmp, "parts", [P, UT, PARTS, D1], BF16)
        step_sum = pair(o.tmp, "step_sum", [P, D1])
        iota = o.psum("iota", [P, 512])
        hot_ps, a_ps, sums = pair(o.psum, "hot_ps", [P, UT, P], BF16), pair(o.psum, "a_ps", [P, UT, D]), pair(o.psum, "sums", [P, 512])
        landed = several(RING, o.sem, "landed")
        iota_set, parts_set, rel_ready, hot_ready, turned, hot_t_ready, expanded, added, first_ready, left_ready, second_ready, third_ready, summed, sum_ready, acc_ready = o.sems(
            "iota_set", "parts_set", "rel_ready", "hot_ready", "turned", "hot_t_ready", "expanded", "added", "first_ready", "left_ready", "second_ready", "third_ready",
            "summed", "sum_ready", "acc_ready")
        block = own.enter_context(nc.Block())

        def step_value(eng, u, row, most):
            return eng.value_load(k.step_row[0:1, bass.ds(u + row * UNIT_COLS * P, 1)], min_val=0, max_val=most)

        def staggered(eng, *stages, rounds=1):
            def body(u, r, used, n):
                for stage, lag in stages:
                    if n >= lag:
                        stage(u - lag, (r - lag) % RING, used if r >= lag else used - 1, n if n == MANY else n - lag)

            in_rings(eng, UNITS, RING, body, rounds)
            for late in range(1, 1 + max(lag for _, lag in stages)):
                for stage, lag in stages:
                    if lag >= late:
                        u = UNITS - 1 + late - lag
                        stage(u, u % RING, u // RING, MANY)

        @block.sync
        def _(sp):
            def body(u, r, used, n):
                unit = step_value(sp, u, 1, NCH * CE // UE - 1)
                if n >= RING:
                    sp.wait_ge(added, u - RING + 1)
                sp.dma_start(edges[r][:], k.sorted.rearrange("(p t) d -> p (t d)", t=UT)[bass.ds(unit * P, P), :]).then_inc(landed[r], 16)

            in_rings(sp, UNITS, RING, body)

        @block.vector
        def _(dve):
            link(dve, dve.tensor_copy(iota[:, 0:W], k.iota[:]), iota_set, 1)
            for p in parts:
                link(dve, dve.memset(p[:], 0.0), parts_set, 2 * parts.index(p) + 1)
                dve.memset(p[:, :, 0, D], 1.0).then_inc(parts_set, 1)
            dve.memset(acc[:], 0.0).then_inc(acc_ready, 1)
            shape = [P, UT, W]

            def make_rel(u, r, used, n):
                dve.wait_ge(landed[r], 16 * (used + 1))
                if n >= SHORT:
                    dve.wait_ge(hot_ready, u - SHORT + 1)
                rows = edges[r][:].rearrange("p (t d) -> p t d", d=D1)
                dve.tensor_scalar(rel[r % SHORT][:], rows[:, :, D], k.step_node[:, bass.ds(u, 1)], None, ALU.subtract).then_inc(rel_ready, 1)

            def make_hot(u, r, used, n):
                dve.wait_ge(rel_ready, u + 1)
                if n >= RING:
                    dve.wait_ge(summed, u - RING + 1)
                dve.tensor_tensor(hot[r][:], wide(iota[:, 0:W], 1, shape), wide(rel[r % SHORT][:], 2, shape), ALU.is_equal).then_inc(hot_ready, 1)

            def add(u, r, used, n):
                dve.wait_ge(expanded, u + 1)
                if n >= SHORT:
                    dve.wait_ge(left_ready, u - SHORT + 1)
                dve.tensor_tensor(total[r % SHORT][:], a_ps[r % 2][:], edges[r][:].rearrange("p (t d) -> p t d", d=D1)[:, :, 0:D], ALU.add).then_inc(added, 1)

            def add_parts(u, r, used, n):
                dve.wait_ge(summed, u + 1)
                if n >= 2:
                    dve.wait_ge(acc_ready, u)
                dve.tensor_reduce(step_sum[r % 2][:], sums[r % 2][:, 0:PARTS * D1].rearrange("p (i d) -> p d i", i=PARTS), AX, ALU.add).then_inc(sum_ready, 1)

            def keep(u, r, used, n):
                part = acc[:, bass.ds(step_value(dve, u, 0, WINDOWS - 1), 1), :].rearrange("p w d -> p (w d)")
                dve.wait_ge(sum_ready, u + 1)
                dve.wait_ge(acc_ready, u + 1)
                dve.tensor_tensor(part, part, step_sum[r % 2][:], ALU.add).then_inc(acc_ready, 1)

            staggered(dve, (make_rel, 0), (add, 3), (make_hot, 0), (keep, 8), (add_parts, 7))
            dve.wait_ge(acc_ready, UNITS + 1)
            inverse_counts(dve, k, sum_ready, UNITS + 1)

        @block.tensor
        def _(pe):
            def turn(u, r, used, n):
                wait_alone(pe, hot_ready, u + 1)
                if n >= 2:
                    wait_alone(pe, hot_t_ready, u - 1)
                for t in range(UT):
                    mm = pe.transpose(hot_ps[r % 2][:, t, :], hot[r][:, t, :], k.ident_b[:])
                mm.then_inc(turned, 1)

            def expand(u, r, used, n):
                window = bass.ds(step_value(pe, u, 0, WINDOWS - 1), 1)
                pe.wait_ge(hot_t_ready, u + 1)
                if n >= 2:
                    pe.wait_ge(added, u - 1)
                for t in range(UT):
                    for i in range(PARTS):
                        mm = pe.matmul(a_ps[r % 2][:, t, :], hot_t[r % 2][:, t, :], k.a_parts[:, window, i, :].rearrange("p w d -> p (w d)"),
                                       start=(i == 0), stop=(i == PARTS - 1))
                mm.then_inc(expanded, 1)

            def sum_up(u, r, used, n):
                pe.wait_ge(third_ready, u + 1)
                if n >= 2:
                    pe.wait_ge(sum_ready, u - 1)
                for t in range(UT):
                    mm = pe.matmul(sums[r % 2][:, 0:PARTS * D1], hot[r][:, t, :], parts[r][:, t].rearrange("p i d -> p (i d)"), start=(t == 0), stop=(t == UT - 1))
                mm.then_inc(summed, 1)

            staggered(pe, (turn, 1), (expand, 2), (sum_up, 6))

        @block.scalar
        def _(act):
            act.wait_ge(parts_set, 2 * RING)

            def turn_back(u, r, used, n):
                act.wait_ge(turned, u + 1)
                if n >= 2:
                    act.wait_ge(expanded, u - 1)
                act.copy(hot_t[r % 2][:], hot_ps[r % 2][:]).then_inc(hot_t_ready, 1)

            def first_part(u, r, used, n):
                act.wait_ge(added, u + 1)
                if n >= RING:
                    act.wait_ge(summed, u - RING + 1)
                act.activation(parts[r][:, :, 0, 0:D], total[r % SHORT][:], ACT.Relu)
                act.activation(total[r % SHORT][:], total[r % SHORT][:], ACT.Relu).then_inc(first_ready, 1)

            def second_part(u, r, used, n):
                act.wait_ge(left_ready, u + 1)
                act.copy(parts[r][:, :, 1, 0:D], left[r % SHORT][:]).then_inc(second_ready, 1)

            staggered(act, (first_part, 4), (second_part, 5), (turn_back, 1), rounds=2)

        @block.gpsimd
        def _(pool):
            def rest_of_first(u, r, used, n):
                pool.wait_ge(first_ready, u + 1)
                if n >= SHORT:
                    pool.wait_ge(third_ready, u - SHORT + 1)
                pool.tensor_tensor(left[r % SHORT][:], total[r % SHORT][:], parts[r][:, :, 0, 0:D], ALU.subtract).then_inc(left_ready, 1)

            def third_part(u, r, used, n):
                pool.wait_ge(second_ready, u + 1)
                pool.tensor_tensor(parts[r][:, :, 2, 0:D], left[r % SHORT][:], parts[r][:, :, 1, 0:D], ALU.subtract).then_inc(third_ready, 1)

            staggered(pool, (rest_of_first, 4), (third_part, 5))


def add_bias(dve, k):
    dve.tensor_tensor(k.x[:], k.x[:], wide(k.conv_b[1][:], 1, [P, WINDOWS, D]), ALU.add)


def inverse_counts(dve, k, sem, value):
    link(dve, dve.tensor_scalar(k.inv_count[:], k.acc[:, 0:WINDOWS, D], 1.0, None, ALU.max), sem, value)
    dve.reciprocal(k.inv_count[:], k.inv_count[:])


def group(g):
    return bass.ds(g * GW, GW)


def program(nc, io, out):
    k = Core()
    shape = [P, GW, D]
    with ExitStack() as ctx:
        constants(nc, ctx, k)
        acc = k.acc

        def feed_norm(dve, stage, g, step):
            return dve.scalar_tensor_tensor(stage[:], k.centred[:, group(g), :], 0.0, wide(k.rstd[:, group(g)], 2, shape), ALU.max, ALU.mult)

        def keep_own(bias):
            def keep(dve, part, g, rows, step):
                return dve.tensor_tensor(k.own[:, group(g), :], part, wide(bias[:], 1, shape), ALU.add)
            return keep

        def feed_mean(dve, stage, g, step):
            link(dve, dve.tensor_tensor(stage[:], acc[:, group(g), 0:D], wide(k.inv_count[:, group(g)], 2, shape), ALU.mult), step, g + 1)
            return dve.tensor_tensor(stage[:], stage[:], k.own[:, group(g), :], ALU.add)

        def keep_x(dve, part, g, rows, step):
            return dve.tensor_tensor(k.x[:, group(g), :], k.x[:, group(g), :], part, ALU.add)

        def feed_sums(dve, stage, g, step):
            return dve.tensor_copy(stage[:], acc[:, group(g), :])

        def keep_out(dve, part, g, rows, step):
            link(dve, dve.tensor_tensor(rows[:], part, wide(k.inv_count[:, group(g)], 2, shape), ALU.mult), step, g + 1)
            return dve.tensor_tensor(rows[:], rows[:], k.x[:, group(g), :], ALU.add)

        with nc.sbuf_tensor("own_part", [P, WINDOWS, D], F32) as k.own:
            with nc.sbuf_tensor("centred", [P, WINDOWS, D], F32) as k.centred:
                setup(nc, k, io)
                project(nc, k, "conv1_in", D, k.conv_w[0], feed_norm, False, k.h_table, keep_own(k.conv_b[0]))
                sum_by_dst(nc, k, "agg1", k.h_table, acc, lambda dve: add_bias(dve, k), Counting)
                plan_units(nc, k)
                project(nc, k, "conv2_in", D, k.conv_w[1], feed_mean, True, k.g_table, keep_x, steps=True)
                sum_by_dst(nc, k, "agg2", k.g_table, acc, lambda dve: None, Ranking)
                second_norm(nc, k, acc)
                project(nc, k, "edge_in", D, k.edge_ends, feed_norm, False, k.b_table, keep_own(k.edge_b1))
            place_edges(nc, k, io["edge_attr_64"])
        sum_by_src(nc, k, acc)
        project(nc, k, "edge_out", D1, k.edge_out, feed_sums, False, None, keep_out, steps=True, out=out)


INS = ["x", "src", "dst", "edge_attr_64", "L0_gnn_W1l", "L0_gnn_W1r", "L0_gnn_b1", "L0_gnn_W2l", "L0_gnn_W2r", "L0_gnn_b2",
       "L1_gnn_W1", "L1_gnn_b1", "L1_gnn_W2", "L1_gnn_b2"]


def kernel(**inputs):
    import numpy as np
    import concourse.bacc as bacc
    from concourse import mybir as mb
    from concourse.bass_utils import run_bass_kernel_spmd

    nc = bacc.Bacc("TRN2", target_bir_lowering=False, num_devices=1)
    arrays, io = {}, {}
    for name in INS:
        a = np.ascontiguousarray(inputs[name])
        arrays[f"in_{name}"] = a
        io[name] = nc.dram_tensor(f"in_{name}", a.shape, mb.dt.from_np(a.dtype), kind="ExternalInput").ap()
    out = nc.dram_tensor("out_0", (N, D), mb.dt.float32, kind="ExternalOutput").ap()
    program(nc, io, out)
    r = run_bass_kernel_spmd(nc, [arrays], core_ids=[0])
    return r.results[0]["out_0"]
```

```python
from contextlib import ExitStack

import concourse.bass as bass
from concourse import mybir

P = 128
N = 12500
E = 200000
D = 64
D1 = D + 1
CH = 8
CE = CH * P
NCH = -(-E // CE)
FULL = E // CE
REST = E - FULL * CE
REST_P = (E - FULL * CE) // CH
HALF = NCH // 2
W = P
W_SHIFT = 7
WINDOWS = N // W + 1
ROWS = WINDOWS * W
LAST = N - (WINDOWS - 1) * W
GW = 7
GROUPS = WINDOWS // GW
UT = 8
UE = UT * P
UE_SHIFT = 10
UNITS = NCH * CE // UE + WINDOWS - 1
UNIT_COLS = -(-UNITS // P)
RING = 8
SHORT = RING // 2
ACT_T = 7
PARTS = 3
EPS = 1e-5
assert GROUPS * GW == WINDOWS and HALF * 2 == NCH and NCH - FULL == 1 and REST_P * CH == E - FULL * CE
assert 1 << W_SHIFT == W and 1 << UE_SHIFT == UE

ALU = mybir.AluOpType
ACT = mybir.ActivationFunctionType
AX = mybir.AxisListType.X
F32 = mybir.dt.float32
BF16 = mybir.dt.bfloat16
I32 = mybir.dt.int32
U32 = mybir.dt.uint32


class Core:
    pass


class Own:

    def __init__(self, nc, own, name):
        self.nc, self.own, self.name, self.all = nc, own, name, []

    def tmp(self, s, shape, dt=F32):
        return self.own.enter_context(self.nc.sbuf_tensor(f"{self.name}_{s}", shape, dt))

    def psum(self, s, shape, dt=F32):
        return self.own.enter_context(self.nc.psum_tensor(f"{self.name}_{s}", shape, dt))

    def sem(self, s):
        self.all.append(self.own.enter_context(self.nc.semaphore(f"{self.name}_{s}")))
        return self.all[-1]

    def clear(self):
        for sem in self.all:
            self.nc.gpsimd.sem_clear(sem)

    def sems(self, *names):
        return [self.sem(s) for s in names]


def several(n, make, s, *a):
    return [make(f"{s}{h}", *a) for h in range(n)]


def pair(make, s, *a):
    return several(2, make, s, *a)


def wait_alone(eng, sem, value):
    if not isinstance(value, int):
        value = eng.to_reg(value)
    eng.wait_ge(sem, 1)
    eng.wait_ge(sem, value)


def link(eng, ins, sem, value):
    ins.then_inc(sem, 1)
    eng.wait_ge(sem, value)


MANY = 1 << 20


def in_rings(eng, count, ring, body, rounds=1):
    for s in range(ring * rounds):
        body(s, s % ring, s // ring, s)
    with eng.Fori(rounds, count // ring) as i:
        for r in range(ring):
            body(ring * i + r, r, i, MANY)
    for s in range(count // ring * ring, count):
        body(s, s % ring, s // ring, MANY)


def windows_of_rows(table):
    return table.rearrange("(w p) d -> p w d", p=P)


def wide(v, n, shape):
    return v.unsqueeze(n).to_broadcast(shape)


def norm_vector(dve, k, s, part_ready, between=None):
    n = WINDOWS // s.parts
    for i in range(s.parts):
        part = slice(i * n, (i + 1) * n)
        part_ready(i, part)
        link(dve, dve.tensor_reduce(s.sum[:, part], k.x[:, part, :], AX, ALU.add), s.step, i + 1)
        dve.scalar_tensor_tensor(k.centred[:, part, :], wide(s.sum[:, part], 2, [P, n, D]), -1.0 / D, k.x[:, part, :],
                                 ALU.mult, ALU.add).then_inc(s.centred, 1)
    if between is not None:
        between()
    for i in range(s.parts):
        part = slice(i * n, (i + 1) * n)
        dve.wait_ge(s.squared, i + 1)
        last = dve.tensor_reduce(s.var[:, part], s.square[:, part, :], AX, ALU.add)
    link(dve, last, s.step, s.parts + 1)
    dve.tensor_scalar(s.var[:], s.var[:], 1.0 / D, EPS, ALU.mult, ALU.add).then_inc(s.var_ready, 1)
    dve.wait_ge(s.root_ready, 1)
    link(dve, dve.reciprocal(s.rough[:], s.root[:]), s.step, s.parts + 2)
    link(dve, dve.tensor_tensor(s.fix[:], s.rough[:], s.rough[:], ALU.mult), s.step, s.parts + 3)
    link(dve, dve.tensor_tensor(s.fix[:], s.fix[:], s.var[:], ALU.mult), s.step, s.parts + 4)
    link(dve, dve.tensor_scalar(s.fix[:], s.fix[:], -0.5, 1.5, ALU.mult, ALU.add), s.step, s.parts + 5)
    dve.tensor_tensor(k.rstd[:], s.rough[:], s.fix[:], ALU.mult)


def norm_scalar(act, k, s, between=None):
    n = WINDOWS // s.parts
    for i in range(s.parts):
        act.wait_ge(s.centred, i + 1)
        act.activation(s.square[:, i * n:(i + 1) * n, :], k.centred[:, i * n:(i + 1) * n, :], ACT.Square).then_inc(s.squared, 1)
    if between is not None:
        between()
    act.wait_ge(s.var_ready, 1)
    act.activation(s.root[:], s.var[:], ACT.Sqrt).then_inc(s.root_ready, 1)


class Norm:

    def __init__(self, k, o):
        self.parts = 7
        self.square = k.own
        self.sum, self.var, self.root, self.rough, self.fix = (o.tmp(t, [P, WINDOWS]) for t in ("sum", "var", "root", "rough", "fix"))
        self.step, self.centred, self.squared, self.var_ready, self.root_ready = o.sems("step", "centred", "squared", "var_ready", "root_ready")


def constants(nc, ctx, k):
    def sb(name, shape, dt=F32):
        return ctx.enter_context(nc.sbuf_tensor(name, shape, dt))

    def dram(name, shape, dt=F32):
        return nc.dram_tensor(name, shape, dt).ap()

    k.ident = sb("ident", [P, P])
    k.ident_b = sb("ident_b", [P, P], BF16)
    k.before = sb("before", [P, P])
    k.ones = sb("ones", [P, P])
    k.before_b, k.ones_b = sb("before_b", [P, P], BF16), sb("ones_b", [P, P], BF16)
    k.iota = sb("iota", [P, W])
    k.window_neg = sb("window_neg", [P, WINDOWS])
    k.tile_before = sb("tile_before", [P, CH, CH])
    k.conv_w = [sb(f"conv{i}_w", [D, 2 * D]) for i in (1, 2)]
    k.conv_b = [sb(f"conv{i}_b", [P, D]) for i in (1, 2)]
    k.edge_ends = sb("edge_ends", [D, 2 * D])
    k.edge_attr_w = sb("edge_attr_w", [P, 2, D])
    k.edge_b1 = sb("edge_b1", [P, D])
    k.edge_out = sb("edge_out", [D1, D])
    k.src = sb("src_f", [P, NCH, CH])
    k.src_window = sb("src_window", [P, NCH, CH])
    k.dst_rel = sb("dst_rel", [P, NCH, CH])
    k.least_rel = sb("least_rel", [P, NCH])
    k.win_row = sb("win_row", [1, 4 * NCH], I32)
    k.x = sb("x", [P, WINDOWS, D])
    k.rstd = sb("rstd", [P, WINDOWS])
    k.acc = sb("acc", [P, WINDOWS + 1, D1])
    k.a_parts = sb("a_parts", [P, WINDOWS, PARTS, D], BF16)
    k.place = sb("place", [P, NCH, CH])
    k.inv_count = sb("inv_count", [P, WINDOWS])
    k.window_edges, k.next_place = sb("window_edges", [P, WINDOWS]), sb("next_place", [P, WINDOWS])
    k.step_row = sb("step_row", [1, 2 * UNIT_COLS * P], I32)
    k.step_no = sb("step_no", [P, UNIT_COLS])
    k.step_node = sb("step_node", [P, UNITS])
    k.h_table, k.g_table = dram("h_table", [ROWS, PARTS * D], BF16), dram("g_table", [ROWS, PARTS * D], BF16)
    k.b_table = dram("b_table", [ROWS + W, PARTS * D], BF16)
    k.sorted = dram("sorted_edges", [NCH * CE, D1])
    k.windows = dram("windows", [5, NCH], I32)
    k.units = dram("units", [2, UNIT_COLS * P], I32)


def setup(nc, k, io):
    with ExitStack() as own:
        o = Own(nc, own, "setup")
        norm = Norm(k, Own(nc, own, "norm0"))
        ids = [o.tmp(f"{s}_ids", [HALF, 2, CE], I32) for s in ("src", "dst")]
        ids_f = [k.acc[0:HALF].rearrange("q w d -> q (w d)")[:, i * 2 * CE:(i + 1) * 2 * CE].rearrange("q (a e) -> q a e", a=2) for i in range(2)]
        zeros, w_rows = o.tmp("zeros", [P, PARTS * D], BF16), o.tmp("w_rows", [D, 4, D])
        least, most, first, last_w, count, span, rel = (o.tmp(s, [HALF, 2], I32) for s in ("least", "most", "first", "last_w", "count", "span", "rel"))
        first_f, least_f, most_f = (o.tmp(s, [HALF, 2]) for s in ("first_f", "least_f", "most_f"))
        rel_i = o.tmp("rel_i", [P, NCH], I32)
        w_ps = o.psum("w_ps", [D, 8, D])
        ids_ps = pair(o.psum, "ids_ps", [P, 4, P])
        pieces = ((0,), (1, 2), (3, 4), (5, 6))
        x_landed = several(len(pieces), o.sem, "x_landed")
        ids_landed = [o.sem(f"{s}_landed") for s in ("src", "dst")]
        cleared, ids_cleared, x_cleared, masks, w_landed, dst_float, src_float, relative, ids_turned, ids_kept = o.sems(
            "cleared", "ids_cleared", "x_cleared", "masks", "w_landed", "dst_float", "src_float", "relative", "ids_turned", "ids_kept")
        windows_made, windows_stored, rel_landed, row_landed, zeros_stored, w_turned, step = o.sems(
            "windows_made", "windows_stored", "rel_landed", "row_landed", "zeros_stored", "w_turned", "step")
        own.callback(o.clear)
        block = own.enter_context(nc.Block())

        @block.sync
        def _(sp):
            full = E // (2 * CE)

            def load_ids(name, to, landed):
                sp.dma_start(to[0:full], io[name][0:full * 2 * CE].rearrange("(q a e) -> q a e", a=2, e=CE)).then_inc(landed, 16)
                sp.dma_start(to[full:HALF, 0, :], io[name][full * 2 * CE:E - REST].rearrange("(a e) -> a e", a=1)).then_inc(landed, 16)
                sp.dma_start(to[full:HALF, 1, 0:REST], io[name][E - REST:E].rearrange("(a e) -> a e", a=1)).then_inc(landed, 16)

            sp.wait_ge(ids_cleared, 1)
            load_ids("dst", ids[1], ids_landed[1])
            sp.wait_ge(x_cleared, 1)
            n = WINDOWS // norm.parts
            x = windows_of_rows(io["x"][0:(WINDOWS - 1) * W, :])
            for i, piece in enumerate(pieces):
                part = slice(piece[0] * n, min((piece[-1] + 1) * n, WINDOWS - 1))
                sp.dma_start(k.x[:, part, :], x[:, part, :]).then_inc(x_landed[i], 16)
            sp.dma_start(k.x[0:LAST, WINDOWS - 1, :], io["x"][(WINDOWS - 1) * W:N, :]).then_inc(x_landed[-1], 16)
            load_ids("src", ids[0], ids_landed[0])
            sp.wait_ge(windows_made, 1)
            for i, w in enumerate((first, count, least, span, rel)):
                sp.dma_start(k.windows[i].rearrange("(q a) -> q a", a=2), w[:]).then_inc(windows_stored, 16)
            sp.wait_ge(windows_stored, 16 * 5)
            sp.dma_start(k.win_row[:], k.windows[0:4, :].rearrange("(o i) c -> o (i c)", o=1)).then_inc(row_landed, 16)
            sp.dma_start(rel_i[:], k.windows[4:5, :].to_broadcast([P, NCH])).then_inc(rel_landed, 16)
            sp.wait_ge(row_landed, 16)

        @block.scalar
        def _(act):
            for i, name in enumerate(("L0_gnn_W1l", "L0_gnn_W1r", "L0_gnn_W2l", "L0_gnn_W2r")):
                act.dma_start(w_rows[:, i, :], io[name]).then_inc(w_landed, 16)
            w1 = io["L1_gnn_W1"]
            for i in range(2):
                act.dma_start(k.edge_ends[:, (1 - i) * D:(2 - i) * D], w1[i * D:(i + 1) * D, :]).then_inc(w_landed, 16)
            for to, name in ((k.conv_b[0], "L0_gnn_b1"), (k.conv_b[1], "L0_gnn_b2"), (k.edge_b1, "L1_gnn_b1")):
                act.dma_start(to[:], io[name].rearrange("(a d) -> a d", a=1).to_broadcast([P, D])).then_inc(w_landed, 16)
            act.dma_start(k.edge_out[0:D, :], io["L1_gnn_W2"]).then_inc(w_landed, 16)
            act.dma_start(k.edge_out[D:D1, :], io["L1_gnn_b2"].rearrange("(a d) -> a d", a=1)).then_inc(w_landed, 16)
            act.wait_ge(cleared, 1)
            for i in range(2):
                act.dma_start(k.edge_attr_w[i * D:(i + 1) * D, i, :], w1[2 * D:3 * D, :]).then_inc(w_landed, 16)
            act.dma_start(k.b_table[ROWS:ROWS + W, :], zeros[:]).then_inc(zeros_stored, 16)
            def keep_ids():
                for g in range(8):
                    i, a, t = g // 4, g // 2 % 2, g % 2 * 4
                    act.wait_ge(ids_turned, g + 1)
                    to = (k.dst_rel, k.src)[i]
                    act.copy(to[:].rearrange("p (q a) t -> p a t q", a=2)[:, a, t:t + 4, :], ids_ps[g % 2][:, :, 0:HALF]).then_inc(ids_kept, 1)

            norm_scalar(act, k, norm, keep_ids)
            act.wait_ge(zeros_stored, 16)
            act.wait_ge(w_landed, 16 * 13)

        @block.gpsimd
        def _(pool):
            pool.iota(k.iota[:], [[1, W]], base=0, channel_multiplier=0, allow_small_or_imprecise_dtypes=True)
            pool.iota(k.window_neg[:], [[-W, WINDOWS]], base=0, channel_multiplier=0, allow_small_or_imprecise_dtypes=True)
            pool.iota(k.step_no[:], [[1, UNIT_COLS]], base=0, channel_multiplier=UNIT_COLS, allow_small_or_imprecise_dtypes=True)
            pool.wait_ge(cleared, 1)
            pool.affine_select(out=k.ident[:], in_=k.ident[:], pattern=[[-1, P]], compare_op=ALU.not_equal, fill=1.0,
                               base=0, channel_multiplier=1).then_inc(masks, 1)
            pool.affine_select(out=k.before[:], in_=k.ones[:], pattern=[[1, P]], compare_op=ALU.is_gt, fill=0.0,
                               base=0, channel_multiplier=-1).then_inc(masks, 1)
            pool.wait_ge(ids_landed[0], 48)
            pool.tensor_copy(ids_f[0][:], ids[0][:]).then_inc(src_float, 1)

        @block.tensor
        def _(pe):
            pe.wait_ge(masks, 2)
            pe.wait_ge(w_landed, 16 * 13)
            for i in range(4):
                mm = pe.transpose(w_ps[:, i, :], w_rows[:, i, :], k.ident[0:D, 0:D])
            mm.then_inc(w_turned, 1)
            for g in range(8):
                i, a, t = g // 4, g // 2 % 2, g % 2 * 4
                if g == 0:
                    pe.wait_ge(relative, 2)
                if g == 4:
                    pe.wait_ge(src_float, 1)
                if g >= 2:
                    pe.wait_ge(ids_kept, g - 1)
                for j in range(4):
                    mm = pe.transpose(ids_ps[g % 2][:, j, 0:HALF], ids_f[1 - i][:, a, :].rearrange("q (p t) -> q t p", t=CH)[:, t + j, :],
                                      k.ident[0:HALF, 0:HALF])
                mm.then_inc(ids_turned, 1)

        @block.vector
        def _(dve):
            for i in range(2):
                last = dve.memset(ids[i][96:HALF, 1, REST:], N)
            last.then_inc(ids_cleared, 1)
            dve.memset(k.x[:, WINDOWS - 1, :], 0.0).then_inc(x_cleared, 1)
            dve.memset(zeros[:], 0.0)
            dve.memset(k.ident[:], 0.0)
            dve.memset(k.ones[:], 1.0)
            dve.memset(k.edge_attr_w[:], 0.0)
            link(dve, dve.memset(k.tile_before[:], 0.0), step, 1)
            for t in range(1, CH):
                dve.memset(k.tile_before[:, t, 0:t], 1.0)
            dve.sem_inc(cleared, 1)
            dst = ids_f[1]
            dve.wait_ge(ids_landed[1], 48)
            link(dve, dve.tensor_copy(dst[:], ids[1][:]), dst_float, 1)
            dve.tensor_reduce(least_f[:], dst[:], AX, ALU.min)
            link(dve, dve.tensor_reduce(most_f[:], dst[:], AX, ALU.max), step, 2)
            dve.tensor_copy(least[:], least_f[:])
            link(dve, dve.tensor_copy(most[:], most_f[:]), step, 3)
            dve.tensor_scalar(first[:], least[:], W_SHIFT, None, ALU.arith_shift_right)
            dve.tensor_scalar(last_w[:], most[:], W_SHIFT, None, ALU.arith_shift_right)
            link(dve, dve.tensor_tensor(span[:], most[:], least[:], ALU.subtract), step, 4)
            dve.tensor_tensor(count[:], last_w[:], first[:], ALU.subtract)
            dve.tensor_scalar(span[:], span[:], W_SHIFT, None, ALU.arith_shift_right)
            link(dve, dve.tensor_scalar(first_f[:], first[:], W, None, ALU.mult), step, 5)
            dve.tensor_scalar(count[:], count[:], 1, None, ALU.add)
            dve.tensor_scalar(span[:], span[:], 1, None, ALU.add)
            dve.tensor_tensor(rel[:], least_f[:], first_f[:], ALU.subtract).then_inc(windows_made, 1)
            for a in range(2):
                dve.tensor_scalar(dst[:, a, :], dst[:, a, :], first_f[:, a:a + 1], None, ALU.subtract).then_inc(relative, 1)
            def part_ready(i, part):
                for j, piece in enumerate(pieces):
                    if i == piece[0]:
                        dve.wait_ge(x_landed[j], 32 if j == len(pieces) - 1 else 16)

            def keep_weights():
                dve.wait_ge(w_turned, 1)
                for i in range(2):
                    dve.tensor_copy(k.conv_w[i][:], w_ps[:, 2 * i:2 * i + 2, :].rearrange("i s o -> i (s o)"))
                for to, mask in ((k.ident_b, k.ident), (k.before_b, k.before), (k.ones_b, k.ones)):
                    dve.tensor_copy(to[:], mask[:])

            norm_vector(dve, k, norm, part_ready, keep_weights)
            dve.wait_ge(rel_landed, 16)
            dve.tensor_copy(k.least_rel[:], rel_i[:])


def project(nc, k, name, depth, weights, feed, relu, table, keep, steps=False, out=None):
    with ExitStack() as own:
        o = Own(nc, own, name)
        cols = weights.shape[-1]
        stage, h_t = pair(o.tmp, "stage", [P, GW, depth]), pair(o.tmp, "h_t", [depth, GW, P])
        rows = pair(o.tmp, "rows", [P, GW, D]) if table is None else pair(o.tmp, "rows", [P, GW, PARTS, D], BF16)
        left = pair(o.tmp, "left", [P, GW, D]) if table is not None else (None, None)
        turn_ps, rows_ps = pair(o.psum, "turn_ps", [P, GW + 1, P]), pair(o.psum, "rows_ps", [P, GW + 1, P])
        staged, turned, h_t_ready, product, kept = o.sems("staged", "turned", "h_t_ready", "product", "kept")
        first_ready, second_ready, rows_ready = o.sems("first_ready", "second_ready", "rows_ready") if table is not None else (None, None, None)
        step = o.sem("step") if steps else None
        stored = pair(o.sem, "stored")
        block = own.enter_context(nc.Block())
        last = GROUPS - 1

        def staggered(eng, *stages):
            def body(g, h, used, n):
                for stage, lag in stages:
                    if n >= lag:
                        stage(g - lag, (h - lag) % 2, used + (h - lag) // 2, n if n == MANY else n - lag)

            in_rings(eng, GROUPS, 2, body, rounds=2)
            for late in range(1, 1 + max(lag for _, lag in stages)):
                for stage, lag in stages:
                    if lag >= late:
                        g = last + late - lag
                        stage(g, g % 2, g // 2, MANY)

        @block.vector
        def _(dve):
            def put(g, h, used, n):
                if n >= 2:
                    dve.wait_ge(turned, g - 1)
                feed(dve, stage[h], g, step).then_inc(staged, 1)

            def take(g, h, used, n):
                if table is None:
                    dve.wait_ge(product, g + 1)
                    if n >= 2:
                        dve.wait_ge(stored[h], 16 * used)
                    keep(dve, rows_ps[h][:, 0:GW, 0:cols], g, rows[h], step).then_inc(kept, 1)
                    return
                dve.wait_ge(first_ready, g + 1)
                dve.tensor_tensor(left[h][:], rows_ps[h][:, 0:GW, 0:D], rows[h][:, :, 0, :], ALU.subtract)
                keep(dve, rows_ps[h][:, 0:GW, D:cols], g, None, step).then_inc(kept, 1)

            def third_part(g, h, used, n):
                dve.wait_ge(second_ready, g + 1)
                dve.tensor_tensor(rows[h][:, :, 2, :], left[h][:], rows[h][:, :, 1, :], ALU.subtract).then_inc(rows_ready, 1)

            if table is None:
                staggered(dve, (put, 0), (take, 2))
            else:
                staggered(dve, (put, 0), (third_part, 3), (take, 2))

        @block.tensor
        def _(pe):
            def turn(g, h, used, n):
                wait_alone(pe, staged, g + 1)
                if n >= 2:
                    wait_alone(pe, h_t_ready, g - 1)
                for i in range(GW):
                    mm = pe.transpose(turn_ps[h][0:depth, i, :], stage[h][:, i, :], k.ident[:])
                mm.then_inc(turned, 1)

            def products(g, h, used, n):
                pe.wait_ge(h_t_ready, g + 1)
                if n >= 2:
                    pe.wait_ge(kept, g - 1)
                for i in range(GW):
                    mm = pe.matmul(rows_ps[h][:, i, 0:cols], h_t[h][:, i, :], weights[:], start=True, stop=True)
                mm.then_inc(product, 1)

            staggered(pe, (turn, 1), (products, 2))

        @block.scalar
        def _(act):
            def turn_back(g, h, used, n):
                act.wait_ge(turned, g + 1)
                if n >= 2:
                    act.wait_ge(product, g - 1)
                act.activation(h_t[h][:], turn_ps[h][0:depth, 0:GW, :], ACT.Relu if relu else ACT.Copy).then_inc(h_t_ready, 1)

            def first_part(g, h, used, n):
                act.wait_ge(product, g + 1)
                if n >= 2:
                    act.wait_ge(stored[h], 16 * used)
                act.copy(rows[h][:, :, 0, :], rows_ps[h][:, 0:GW, 0:D]).then_inc(first_ready, 1)

            def second_part(g, h, used, n):
                act.wait_ge(kept, g + 1)
                act.copy(rows[h][:, :, 1, :], left[h][:]).then_inc(second_ready, 1)

            if table is None:
                staggered(act, (turn_back, 1))
            else:
                staggered(act, (turn_back, 1), (second_part, 3), (first_part, 2))

        @block.sync
        def _(sp):
            to = windows_of_rows(out[0:(WINDOWS - 1) * W, :] if out is not None else table[0:ROWS, :])

            def body(g, h, used, n):
                sp.wait_ge(kept if table is None else rows_ready, g + 1)
                if out is not None and isinstance(g, int) and g == last:
                    sp.dma_start(to[:, g * GW:WINDOWS - 1, :], rows[h][:, 0:GW - 1, :]).then_inc(stored[h], 16)
                    sp.dma_start(out[(WINDOWS - 1) * W:N, :], rows[h][0:LAST, GW - 1, :]).then_inc(stored[h], 16)
                else:
                    sp.dma_start(to[:, bass.ds(g * GW, GW), :], rows[h][:] if table is None else rows[h][:].rearrange("p w i d -> p w (i d)")).then_inc(stored[h], 16)

            for g in range(2):
                body(g, g, 0, g)
            with sp.Fori(1, GROUPS // 2 - 1) as i:
                for h in range(2):
                    body(2 * i + h, h, i, MANY)
            for g in (last - 1, last):
                body(g, g % 2, g // 2, MANY)
            for h in range(2):
                sp.wait_ge(stored[h], 16 * (GROUPS // 2) + (16 if out is not None and h == last % 2 else 0))


def sum_by_dst(nc, k, name, table, acc, before_edges, sorting):
    with ExitStack() as own:
        o = Own(nc, own, name)
        rows, one_hot = o.tmp("rows", [P, 2, CH, PARTS * D + 1], BF16), o.tmp("one_hot", [P, 2, 2, CH, W], BF16)
        index, shifted = pair(o.tmp, "index", [P, CH], U32), o.tmp("shifted", [P, CH])
        more_hot = o.tmp("more_hot", [P, CH, W], BF16)
        s = sorting(k, o)
        iota = o.psum("iota", [P, 512])
        sums, more_sums = pair(o.psum, "sums", [P, 4, P]), o.psum("more_sums", [P, 512])
        index_ready, landed, rows_used = (pair(o.sem, t) for t in ("index_ready", "landed", "rows_used"))
        begun, hot_ready, product, added, shift_done, more_ready, more_product, more_added, more_shifted = o.sems(
            "begun", "hot_ready", "product", "added", "shift_done", "more_ready", "more_product", "more_added", "more_shifted")
        block = own.enter_context(nc.Block())

        @block.gpsimd
        def _(pool):
            pool.wait_ge(begun, 1)
            with pool.Fori(0, NCH // 2) as i:
                for h in range(2):
                    wait_alone(pool, index_ready[h], i + 1)
                    for t in range(CH):
                        pool.indirect_dma_start(rows[:, h, t, 0:PARTS * D], None, table,
                                                bass.IndirectOffsetOnAxis(ap=index[h][:, t:t + 1], axis=0)).then_inc(landed[h], 16)

        @block.scalar
        def _(act):
            def put_index(c, h):
                act.copy(index[h][:], k.src[:, bass.ds(c, 1), :].rearrange("p c t -> p (c t)")).then_inc(index_ready[h], 1)

            for h in range(2):
                put_index(h, h)
            with act.Fori(1, NCH // 2) as i:
                for h in range(2):
                    act.wait_ge(rows_used[h], i)
                    put_index(2 * i + h, h)

        @block.tensor
        def _(pe):
            s.begin_tensor(pe)
            windows = pe.alloc_register(f"{name}_pe_windows")
            pe.reg_mov(windows, 0)

            def add_up(to, hot, h):
                for i in (2, 0, 1):
                    n = D1 if i == 2 else D
                    for t in range(CH):
                        mm = pe.matmul(to[:, 0:n], hot[:, t, :], rows[:, h, t, i * D:i * D + n], start=(i == 2 and t == 0), stop=(i == 1 and t == CH - 1), skip_group_check=True)
                return mm

            def chunk(c, h, used, first):
                count = pe.value_load(k.win_row[0:1, bass.ds(NCH + c, 1)], min_val=1, max_val=WINDOWS)
                s.prefix(pe, c, h)
                wait_alone(pe, landed[h], 16 * CH * (used + 1))
                pe.wait_ge(hot_ready, c + 1)
                if not first:
                    pe.wait_ge(added, c - 1)
                for w in range(2):
                    mm = add_up(sums[h][:, w, :], one_hot[:, h, w], h)
                mm.then_inc(product, 1)
                with pe.If(count > 2):
                    with pe.Fori(2, count):
                        pe.reg_add(windows, windows, 1)
                        pe.wait_ge(more_ready, pe.snap(windows, min_val=1, max_val=NCH * WINDOWS))
                        add_up(more_sums, more_hot, h).then_inc(more_product, 1)

            for h in range(2):
                chunk(h, h, 0, True)
            with pe.Fori(1, NCH // 2) as i:
                for h in range(2):
                    chunk(2 * i + h, h, i, False)

        @block.vector
        def _(dve):
            dve.memset(rows[:], 1.0).then_inc(begun, 1)
            dve.tensor_copy(iota[:, 0:W], k.iota[:]).then_inc(begun, 1)
            link(dve, dve.memset(acc[:], 0.0), begun, 3)
            before_edges(dve)
            s.begin(dve)
            windows, first = dve.alloc_register(f"{name}_dve_windows"), dve.alloc_register(f"{name}_dve_first")
            dve.reg_mov(windows, 0)
            shape = [P, CH, W]

            def make_hot(to, rel):
                return dve.tensor_tensor(to, wide(iota[:, 0:W], 1, shape), wide(rel, 2, shape), ALU.is_equal)

            def shift(rel, w):
                return dve.tensor_scalar(shifted[:], rel, k.window_neg[:, bass.ds(w, 1)], None, ALU.add)

            def node_rows(at, n):
                return acc[:, bass.ds(at, n), :]

            def make(c, h):
                rel = k.dst_rel[:, bass.ds(c, 1), :].rearrange("p c t -> p (c t)")
                if not (isinstance(c, int) and c == 0):
                    dve.wait_ge(hot_ready, c)
                link(dve, shift(rel, 1), shift_done, c + 1)
                make_hot(one_hot[:, h, 0], rel)
                make_hot(one_hot[:, h, 1], shifted[:]).then_inc(hot_ready, 1)

            def windows_of(c):
                count = dve.value_load(k.win_row[0:1, bass.ds(c + NCH, 1)], min_val=1, max_val=WINDOWS)
                return count, dve.value_load(k.win_row[0:1, bass.ds(c, 1)], min_val=0, max_val=WINDOWS - 1)

            def add(c, h, count, base):
                part = node_rows(base, 2)
                dve.wait_ge(product, c + 1)
                if not (isinstance(c, int) and c == 0):
                    dve.wait_ge(added, c)
                dve.tensor_tensor(part, part, sums[h][:, 0:2, 0:D1], ALU.add).then_inc(added, 1)
                dve.reg_mov(first, base)
                with dve.If(count > 2):
                    with dve.Fori(2, count) as w:
                        dve.reg_add(windows, windows, 1)
                        number = dve.snap(windows, min_val=1, max_val=NCH * WINDOWS)
                        more = node_rows(dve.snap(first, min_val=0, max_val=WINDOWS - 3) + 2, 1).rearrange("p w d -> p (w d)")
                        dve.wait_ge(hot_ready, c + 1 if isinstance(c, int) and c == NCH - 1 else c + 2)
                        dve.wait_ge(added, c + 1)
                        link(dve, shift(k.dst_rel[:, bass.ds(c, 1), :].rearrange("p c t -> p (c t)"), w), more_shifted, number)
                        make_hot(more_hot[:], shifted[:]).then_inc(more_ready, 1)
                        dve.wait_ge(more_product, number)
                        link(dve, dve.tensor_tensor(more, more, more_sums[:, 0:D1], ALU.add), more_added, number)
                        dve.reg_add(first, first, 1)
                dve.sem_inc(rows_used[h], 1)

            def both(c, h):
                make(c, h)
                count, base = windows_of(c - 1)
                s.members(dve, c, h)
                add(c - 1, 1 - h, count, base)
                s.sort(dve, c, h)

            make(0, 0)
            s.members(dve, 0, 0)
            s.sort(dve, 0, 0)
            both(1, 1)
            with dve.Fori(1, NCH // 2) as i:
                both(2 * i, 0)
                both(2 * i + 1, 1)
            add(NCH - 1, 1, *windows_of(NCH - 1))
            dve.wait_ge(added, NCH)
            s.end(dve)

        if sorting is Ranking:
            @block.sync
            def _(sp):
                s.store_steps(sp)


class Counting:

    def __init__(self, k, o):
        self.k, self.member, self.edges = k, o.tmp("member", [P, WINDOWS, CH]), o.tmp("edges", [P, WINDOWS])
        self.same, self.window_i = o.tmp("same", [P, CH, CH]), o.tmp("window_i", [P, NCH, CH], I32)
        self.step = o.sem("sort_step")

    def begin_tensor(self, pe):
        pass

    def prefix(self, pe, c, h):
        pass

    def begin(self, dve):
        dve.memset(self.k.window_edges[:], 0.0)
        link(dve, dve.tensor_copy(self.window_i[:], self.k.src[:]), self.step, 1)
        link(dve, dve.tensor_scalar(self.window_i[:], self.window_i[:], W_SHIFT, None, ALU.arith_shift_right), self.step, 2)
        link(dve, dve.tensor_copy(self.k.src_window[:], self.window_i[:]), self.step, 3)

    def end(self, dve):
        inverse_counts(dve, self.k, self.step, 5 * NCH + 4)

    def members(self, dve, c, h):
        shape = [P, WINDOWS, CH]
        link(dve, dve.tensor_tensor(self.member[:], wide(self.k.iota[:, 0:WINDOWS], 2, shape),
                                    self.k.src_window[:, bass.ds(c, 1), :].to_broadcast(shape), ALU.is_equal), self.step, 5 * c + 4)
        dve.tensor_reduce(self.edges[:], self.member[:], AX, ALU.add).then_inc(self.step, 1)

    def sort(self, dve, c, h):
        k, shape = self.k, [P, CH, CH]
        window = k.src_window[:, bass.ds(c, 1), :].rearrange("p c t -> p (c t)")
        link(dve, dve.tensor_tensor(self.same[:], wide(window, 2, shape), wide(window, 1, shape), ALU.is_equal), self.step, 5 * c + 6)
        dve.tensor_tensor(k.window_edges[:], k.window_edges[:], self.edges[:], ALU.add)
        link(dve, dve.tensor_tensor(self.same[:], self.same[:], k.tile_before[:], ALU.mult), self.step, 5 * c + 7)
        link(dve, dve.tensor_reduce(k.place[:, bass.ds(c, 1), :].rearrange("p c t -> p (c t)"), self.same[:], AX, ALU.add), self.step, 5 * c + 8)


class Ranking:

    def __init__(self, k, o):
        self.k, self.member = k, pair(o.tmp, "member", [P, CH, WINDOWS], BF16)
        self.places, self.chosen, self.first = o.tmp("places", [P, WINDOWS]), o.tmp("chosen", [P, CH, WINDOWS]), o.tmp("first", [P, CH])
        self.before_ps = o.psum("before_ps", [P, 4, P])
        self.total, self.totals, self.start_f, self.own_step = o.tmp("total", [WINDOWS, 1]), o.tmp("totals", [WINDOWS, P]), o.tmp("start_f", [P, WINDOWS]), o.tmp("own_step", [P, WINDOWS])
        self.start_i, self.not_past = o.tmp("start_i", [P, WINDOWS], I32), o.tmp("not_past", [P, UNIT_COLS, WINDOWS - 1])
        self.window, self.window_i, self.unit_i = o.tmp("window", [P, UNIT_COLS]), o.tmp("window_i", [P, UNIT_COLS], I32), o.tmp("unit_i", [P, UNIT_COLS], I32)
        self.window_all = o.tmp("window_all", [P, UNIT_COLS * P], I32)
        self.members_ready, self.before_ready, self.step = o.sems("members_ready", "before_ready", "sort_step")
        self.summed, self.total_ready, self.started, self.steps_made, self.planned, self.stored, self.landed = o.sems(
            "summed", "total_ready", "started", "steps_made", "planned", "stored", "steps_landed")

    def begin_tensor(self, pe):
        k, ps = self.k, self.before_ps
        pe.matmul(ps[0:WINDOWS, 2, 0:1], k.window_edges[:], k.ones[:, 0:1], start=True, stop=True).then_inc(self.summed, 1)
        pe.wait_ge(self.total_ready, 1)
        pe.matmul(ps[:, 3, 0:WINDOWS], self.totals[:], k.before[0:WINDOWS, 0:WINDOWS], start=True, stop=True).then_inc(self.started, 1)

    def prefix(self, pe, c, h):
        pe.wait_ge(self.members_ready, c + 1)
        for i, mask in enumerate((self.k.before_b, self.k.ones_b)):
            for t in range(CH):
                mm = pe.matmul(self.before_ps[:, i, 0:WINDOWS], mask[:], self.member[h][:, t, :], start=(t == 0), stop=(t == CH - 1))
        mm.then_inc(self.before_ready, 1)

    def begin(self, dve):
        k, ps, made = self.k, self.before_ps, self.planned
        dve.wait_ge(self.summed, 1)
        link(dve, dve.tensor_copy(self.total[:], ps[0:WINDOWS, 2, 0:1]), made, 1)
        dve.tensor_scalar(self.totals[:], k.ones[0:WINDOWS, :], self.total[:, 0:1], None, ALU.mult).then_inc(self.total_ready, 1)
        dve.wait_ge(self.started, 1)
        dve.tensor_copy(k.next_place[:], ps[:, 3, 0:WINDOWS])
        link(dve, dve.tensor_copy(self.start_i[:], ps[:, 3, 0:WINDOWS]), made, 2)
        link(dve, dve.tensor_scalar(self.start_i[:], self.start_i[:], UE_SHIFT, None, ALU.arith_shift_right), made, 3)
        link(dve, dve.tensor_copy(self.start_f[:], self.start_i[:]), made, 4)
        link(dve, dve.tensor_tensor(self.own_step[:], self.start_f[:], k.iota[:, 0:WINDOWS], ALU.add), made, 5)
        shape = [P, UNIT_COLS, WINDOWS - 1]
        link(dve, dve.tensor_tensor(self.not_past[:], wide(self.own_step[:, 1:WINDOWS], 1, shape), wide(k.step_no[:], 2, shape), ALU.is_le), made, 6)
        link(dve, dve.tensor_reduce(self.window[:], self.not_past[:], AX, ALU.add), made, 7)
        dve.tensor_copy(self.window_i[:], self.window[:])
        dve.tensor_tensor(self.unit_i[:], k.step_no[:], self.window[:], ALU.subtract).then_inc(self.steps_made, 1)

    def store_steps(self, sp):
        k = self.k
        sp.wait_ge(self.steps_made, 1)
        for i, v in enumerate((self.window_i, self.unit_i)):
            sp.dma_start(k.units[i].rearrange("(p a) -> p a", p=P), v[:]).then_inc(self.stored, 16)
        sp.wait_ge(self.stored, 32)
        sp.dma_start(k.step_row[:], k.units.rearrange("(o i) u -> o (i u)", o=1)).then_inc(self.landed, 16)
        sp.dma_start(self.window_all[:], k.units[0:1, :].to_broadcast([P, UNIT_COLS * P])).then_inc(self.landed, 16)
        sp.wait_ge(self.landed, 32)

    def end(self, dve):
        dve.wait_ge(self.landed, 32)
        dve.tensor_scalar(self.k.step_node[:], self.window_all[:, 0:UNITS], W, None, ALU.mult)

    def members(self, dve, c, h):
        shape = [P, CH, WINDOWS]
        dve.tensor_tensor(self.member[h][:], wide(self.k.iota[:, 0:WINDOWS], 1, shape),
                          wide(self.k.src_window[:, bass.ds(c, 1), :].rearrange("p c t -> p (c t)"), 2, shape), ALU.is_equal).then_inc(self.members_ready, 1)

    def sort(self, dve, c, h):
        k = self.k
        dve.wait_ge(self.before_ready, c + 1)
        link(dve, dve.tensor_tensor(self.places[:], self.before_ps[:, 0, 0:WINDOWS], k.next_place[:], ALU.add), self.step, 5 * c + 1)
        link(dve, dve.tensor_tensor(self.chosen[:], self.member[h][:], wide(self.places[:], 1, [P, CH, WINDOWS]), ALU.mult), self.step, 5 * c + 2)
        dve.tensor_tensor(k.next_place[:], self.before_ps[:, 1, 0:WINDOWS], k.next_place[:], ALU.add).then_inc(self.step, 1)
        link(dve, dve.tensor_reduce(self.first[:], self.chosen[:], AX, ALU.add), self.step, 5 * c + 4)
        place = k.place[:, bass.ds(c, 1), :].rearrange("p c t -> p (c t)")
        link(dve, dve.tensor_tensor(place, place, self.first[:], ALU.add), self.step, 5 * c + 5)


def second_norm(nc, k, acc):
    with ExitStack() as own:
        o = Own(nc, own, "norm1")
        norm, mean_ready, x_ready = Norm(k, o), o.sem("mean_ready"), o.sem("x_ready")
        block = own.enter_context(nc.Block())

        @block.vector
        def _(dve):
            def part_ready(i, part):
                dve.wait_ge(mean_ready, i + 1)
                link(dve, dve.tensor_tensor(k.x[:, part, :], k.x[:, part, :], norm.square[:, part, :], ALU.add), x_ready, i + 1)

            norm_vector(dve, k, norm, part_ready)

        @block.gpsimd
        def _(pool):
            n = WINDOWS // norm.parts
            for i in range(norm.parts):
                part = slice(i * n, (i + 1) * n)
                pool.tensor_tensor(norm.square[:, part, :], acc[:, part, 0:D], wide(k.inv_count[:, part], 2, [P, n, D]), ALU.mult).then_inc(mean_ready, 1)

        @block.scalar
        def _(act):
            norm_scalar(act, k, norm)


def place_edges(nc, k, edge_attr):
    with ExitStack() as own:
        o = Own(nc, own, "place")
        attr, b_win, index = pair(o.tmp, "attr", [P, CH * D]), pair(o.tmp, "b_win", [W, PARTS * D], BF16), pair(o.tmp, "index", [P, CH], U32)
        more_rows, further_hot = o.tmp("more_rows", [W, PARTS * D], BF16), o.tmp("further_hot", [P, CH, W], BF16)
        hot, hot_t, rows = pair(o.tmp, "hot", [P, CH, W], BF16), pair(o.tmp, "hot_t", [W, CH, P], BF16), pair(o.tmp, "rows", [P, CH, D1])
        attr_t, rel, shifted = pair(o.tmp, "attr_t", [P, CH // 2, P]), pair(o.tmp, "rel", [P, CH]), o.tmp("shifted", [P, CH])
        left = pair(o.tmp, "left", [P, D])
        iota, rows_ps = o.psum("iota", [P, 512]), pair(o.psum, "rows_ps", [P, CH, D])
        attr_ps, hot_ps = pair(o.psum, "attr_ps", [P, CH // 2, P]), pair(o.psum, "hot_ps", [P, CH, P], BF16)
        loaded, b_landed, scattered = (pair(o.sem, s) for s in ("loaded", "b_landed", "scattered"))
        iota_set, rel_ready, hot_ready, turned, attr_ready, hot_t_ready, first_done, product = o.sems(
            "iota_set", "rel_ready", "hot_ready", "turned", "attr_ready", "hot_t_ready", "first_done", "product")
        more_landed, more_shifted, more_hot, more_turned, more_ready, more_done = o.sems(
            "more_landed", "more_shifted", "more_hot", "more_turned", "more_ready", "more_done")
        rows_ready, src_ready, index_ready, split = o.sems("rows_ready", "src_ready", "index_ready", "split")
        block = own.enter_context(nc.Block())

        def in_turn(eng, ahead, rest):
            def both(c, h, used, n):
                ahead(c, h, used, n)
                if n >= 1:
                    rest(c - 1, 1 - h, used - 1 + h, n - 1)

            for c in range(4):
                both(c, c % 2, c // 2, c)
            with eng.Fori(2, NCH // 2 - 1) as i:
                for h in range(2):
                    both(2 * i + h, h, i, MANY)
            for c in (NCH - 2, NCH - 1):
                both(c, c % 2, c // 2, MANY)
            rest(NCH - 1, 1, NCH // 2 - 1, MANY)

        def further_windows(eng, c, body):
            count = eng.value_load(k.win_row[0:1, bass.ds(c + 3 * NCH, 1)], min_val=1, max_val=WINDOWS)
            with eng.If(count > 1):
                with eng.Fori(1, count) as w:
                    eng.reg_add(number[eng], number[eng], 1)
                    body(w, eng.snap(number[eng], min_val=1, max_val=NCH * WINDOWS))

        number = {}

        def count_further(eng, s):
            number[eng] = eng.alloc_register(f"place_{s}_further")
            eng.reg_mov(number[eng], 0)

        @block.sync
        def _(sp):
            count_further(sp, "sp")
            at = sp.alloc_register("place_sp_at")

            def least_of(c):
                return sp.value_load(k.win_row[0:1, bass.ds(c + 2 * NCH, 1)], min_val=0, max_val=N)

            def load(c, h, used, n):
                least = least_of(c)
                if n >= 2:
                    sp.wait_ge(turned, c - 1)
                if isinstance(c, int) and c == NCH - 1:
                    sp.dma_start(attr[h][0:REST_P, :], edge_attr[FULL * CE:E, :].rearrange("(p t) d -> p (t d)", t=CH)).then_inc(loaded[h], 16)
                else:
                    sp.dma_start(attr[h][:], edge_attr.rearrange("(p t) d -> p (t d)", t=CH)[bass.ds(c * P, P), :]).then_inc(loaded[h], 16)
                if n >= 2:
                    sp.wait_ge(first_done, c - 1)
                sp.dma_start(b_win[h][:], k.b_table[bass.ds(least, W), :]).then_inc(b_landed[h], 16)

            def further(c, h, used, n):
                sp.reg_mov(at, least_of(c))

                def window(w, number):
                    sp.wait_ge(more_hot, number)
                    sp.reg_add(at, at, W)
                    sp.dma_start(more_rows[:], k.b_table[bass.ds(sp.snap(at, min_val=0, max_val=N), W), :]).then_inc(more_landed, 16)

                further_windows(sp, c, window)

            in_turn(sp, load, further)

        @block.gpsimd
        def _(pool):
            def ahead(c, h, used, n):
                wait_alone(pool, rows_ready, c + 1)
                wait_alone(pool, src_ready, c + 1)
                wait_alone(pool, index_ready, c + 1)
                for t in range(CH):
                    pool.indirect_dma_start(k.sorted, bass.IndirectOffsetOnAxis(ap=index[h][:, t:t + 1], axis=0), rows[h][:, t, :], None).then_inc(scattered[h], 16)

            in_turn(pool, ahead, lambda c, h, used, n: None)
            for h in range(2):
                pool.wait_ge(scattered[h], 16 * CH * (NCH // 2))

        @block.tensor
        def _(pe):
            count_further(pe, "pe")

            def turn_hot(h, one_hot):
                for t in range(CH):
                    mm = pe.transpose(hot_ps[h][:, t, :], one_hot[:, t, :], k.ident_b[:])
                return mm

            def add_b(h, b):
                for t in range(CH):
                    for i in range(PARTS):
                        mm = pe.matmul(rows_ps[h][:, t, :], hot_t[h][:, t, :], b[:, i * D:(i + 1) * D], start=False,
                                       stop=(t == CH - 1 and i == PARTS - 1), skip_group_check=True)
                return mm

            def turn(c, h, used, n):
                wait_alone(pe, loaded[h], 16 * (used + 1))
                wait_alone(pe, hot_ready, c + 1)
                if n >= 2:
                    wait_alone(pe, hot_t_ready, c - 1)
                for j in range(CH // 2):
                    pe.transpose(attr_ps[h][:, j, :], attr[h][:, j * P:(j + 1) * P], k.ident[:])
                turn_hot(h, hot[h]).then_inc(turned, 1)

            def products(c, h, used, n):
                pe.wait_ge(attr_ready, c + 1)
                if n >= 2:
                    pe.wait_ge(rows_ready, c - 1)
                for t in range(CH):
                    pe.matmul(rows_ps[h][:, t, :], attr_t[h][:, t // 2, :], k.edge_attr_w[:, t % 2, :], start=(t == 0), stop=False, skip_group_check=True)
                pe.wait_ge(hot_t_ready, c + 1)
                wait_alone(pe, b_landed[h], 16 * (used + 1))
                add_b(h, b_win[h]).then_inc(first_done, 1)

                def window(w, number):
                    wait_alone(pe, more_hot, number)
                    turn_hot(h, further_hot).then_inc(more_turned, 1)
                    pe.wait_ge(more_ready, number)
                    wait_alone(pe, more_landed, number * 16)
                    add_b(h, more_rows).then_inc(more_done, 1)

                further_windows(pe, c, window)
                pe.wait_ge(first_done, c + 1)
                pe.wait_ge(more_done, pe.snap(number[pe], min_val=0, max_val=NCH * WINDOWS) + 1)
                pe.sem_inc(product, 1)

            in_turn(pe, turn, products)

        @block.scalar
        def _(act):
            count_further(act, "act")

            def turned_back(c, h, used, n):
                act.wait_ge(turned, c + 1)
                if n >= 2:
                    act.wait_ge(product, c - 1)
                act.copy(attr_t[h][:], attr_ps[h][:]).then_inc(attr_ready, 1)
                act.copy(hot_t[h][:], hot_ps[h][:]).then_inc(hot_t_ready, 1)

            def rest(c, h, used, n):
                def window(w, number):
                    act.wait_ge(more_turned, number)
                    act.copy(hot_t[h][:], hot_ps[h][:]).then_inc(more_ready, 1)

                further_windows(act, c, window)
                act.wait_ge(product, c + 1)
                if n >= 2:
                    act.wait_ge(scattered[h], 16 * CH * used)
                act.copy(index[h][:], k.place[:, bass.ds(c, 1), :].rearrange("p c t -> p (c t)")).then_inc(index_ready, 1)
                act.copy(rows[h][:, :, 0:D], rows_ps[h][:]).then_inc(rows_ready, 1)

            in_turn(act, turned_back, rest)

        @block.vector
        def _(dve):
            count_further(dve, "dve")
            link(dve, dve.tensor_copy(iota[:, 0:W], k.iota[:]), iota_set, 1)
            dve.sem_inc(more_done, 1)
            shape = [P, CH, W]

            def make_hot(to, offset):
                return dve.tensor_tensor(to[:], wide(iota[:, 0:W], 1, shape), wide(offset[:], 2, shape), ALU.is_equal)

            def split_window(w):
                def part(i):
                    return k.a_parts[:, bass.ds(w, 1), i, :].rearrange("p w d -> p (w d)")

                a = k.own[:, bass.ds(w, 1), :].rearrange("p w d -> p (w d)")
                link(dve, dve.tensor_copy(part(0), a), split, 4 * w + 1)
                link(dve, dve.tensor_tensor(left[0][:], a, part(0), ALU.subtract), split, 4 * w + 2)
                link(dve, dve.tensor_copy(part(1), left[0][:]), split, 4 * w + 3)
                link(dve, dve.tensor_tensor(part(2), left[0][:], part(1), ALU.subtract), split, 4 * w + 4)

            def ahead(c, h, used, n):
                if n >= 2:
                    dve.wait_ge(turned, c - 1)
                link(dve, dve.tensor_scalar(rel[h][:], k.dst_rel[:, bass.ds(c, 1), :].rearrange("p c t -> p (c t)"), k.least_rel[:, bass.ds(c, 1)], None, ALU.subtract),
                     rel_ready, c + 1)
                make_hot(hot[h], rel[h]).then_inc(hot_ready, 1)
                if h == 0:
                    split_window(used)

            def rest(c, h, used, n):
                def window(w, number):
                    dve.wait_ge(first_done, c + 1)
                    dve.wait_ge(more_done, number)
                    link(dve, dve.tensor_scalar(shifted[:], rel[h][:], k.window_neg[:, bass.ds(w, 1)], None, ALU.add), more_shifted, number)
                    make_hot(further_hot, shifted).then_inc(more_hot, 1)

                further_windows(dve, c, window)
                if n >= 2:
                    dve.wait_ge(scattered[h], 16 * CH * used)
                dve.tensor_copy(rows[h][:, :, D], k.src[:, bass.ds(c, 1), :].rearrange("p c t -> p (c t)")).then_inc(src_ready, 1)

            in_turn(dve, ahead, rest)


def sum_by_src(nc, k, acc):
    with ExitStack() as own:
        o = Own(nc, own, "by_src")
        edges, rel = several(RING, o.tmp, "edges", [P, UT * D1]), several(SHORT, o.tmp, "rel", [P, UT])
        hot, hot_t = several(RING, o.tmp, "hot", [P, UT, W], BF16), pair(o.tmp, "hot_t", [W, UT, P], BF16)
        total, left = (several(SHORT, o.tmp, s, [P, UT, D]) for s in ("total", "left"))
        parts = several(RING, o.tmp, "parts", [P, UT, PARTS, D1], BF16)
        step_sum = pair(o.tmp, "step_sum", [P, D1])
        iota = o.psum("iota", [P, 512])
        hot_ps, a_ps, sums = pair(o.psum, "hot_ps", [P, UT, P], BF16), pair(o.psum, "a_ps", [P, UT, D]), pair(o.psum, "sums", [P, 512])
        landed = several(RING, o.sem, "landed")
        iota_set, parts_set, rel_ready, hot_ready, turned, hot_t_ready, expanded, added, last_ready, first_ready, left_ready, second_ready, third_ready, summed, sum_ready, acc_ready = o.sems(
            "iota_set", "parts_set", "rel_ready", "hot_ready", "turned", "hot_t_ready", "expanded", "added", "last_ready", "first_ready", "left_ready", "second_ready", "third_ready",
            "summed", "sum_ready", "acc_ready")
        block = own.enter_context(nc.Block())

        def step_value(eng, u, row, most):
            return eng.value_load(k.step_row[0:1, bass.ds(u + row * UNIT_COLS * P, 1)], min_val=0, max_val=most)

        def staggered(eng, *stages, rounds=1):
            def body(u, r, used, n):
                for stage, lag in stages:
                    if n >= lag:
                        stage(u - lag, (r - lag) % RING, used if r >= lag else used - 1, n if n == MANY else n - lag)

            in_rings(eng, UNITS, RING, body, rounds)
            for late in range(1, 1 + max(lag for _, lag in stages)):
                for stage, lag in stages:
                    if lag >= late:
                        u = UNITS - 1 + late - lag
                        stage(u, u % RING, u // RING, MANY)

        @block.sync
        def _(sp):
            def body(u, r, used, n):
                unit = step_value(sp, u, 1, NCH * CE // UE - 1)
                if n >= RING:
                    sp.wait_ge(added, u - RING + 1)
                sp.dma_start(edges[r][:], k.sorted.rearrange("(p t) d -> p (t d)", t=UT)[bass.ds(unit * P, P), :]).then_inc(landed[r], 16)

            in_rings(sp, UNITS, RING, body)

        @block.vector
        def _(dve):
            link(dve, dve.tensor_copy(iota[:, 0:W], k.iota[:]), iota_set, 1)
            for p in parts:
                dve.memset(p[:, :, 0, D], 1.0)
                dve.memset(p[:, :, 1:PARTS, D], 0.0).then_inc(parts_set, 1)
            shape = [P, UT, W]

            def make_rel(u, r, used, n):
                dve.wait_ge(landed[r], 16 * (used + 1))
                if n >= SHORT:
                    dve.wait_ge(hot_ready, u - SHORT + 1)
                rows = edges[r][:].rearrange("p (t d) -> p t d", d=D1)
                dve.tensor_scalar(rel[r % SHORT][:], rows[:, :, D], k.step_node[:, bass.ds(u, 1)], None, ALU.subtract).then_inc(rel_ready, 1)

            def make_hot(u, r, used, n):
                dve.wait_ge(rel_ready, u + 1)
                if n >= RING:
                    dve.wait_ge(summed, u - RING + 1)
                dve.tensor_tensor(hot[r][:], wide(iota[:, 0:W], 1, shape), wide(rel[r % SHORT][:], 2, shape), ALU.is_equal).then_inc(hot_ready, 1)

            def add(u, r, used, n):
                dve.wait_ge(expanded, u + 1)
                if n >= SHORT:
                    dve.wait_ge(left_ready, u - SHORT + 1)
                dve.tensor_tensor(total[r % SHORT][:], a_ps[r % 2][:], edges[r][:].rearrange("p (t d) -> p t d", d=D1)[:, :, 0:D], ALU.add).then_inc(added, 1)

            def relu_last(u, r, used, n):
                dve.wait_ge(added, u + 1)
                if n >= SHORT:
                    dve.wait_ge(third_ready, u - SHORT + 1)
                dve.tensor_scalar(left[r % SHORT][:, ACT_T:UT, :], total[r % SHORT][:, ACT_T:UT, :], 0.0, None, ALU.max).then_inc(last_ready, 1)

            def add_parts(u, r, used, n):
                dve.wait_ge(summed, u + 1)
                if n >= 2:
                    dve.wait_ge(acc_ready, u)
                dve.tensor_reduce(step_sum[r % 2][:], sums[r % 2][:, 0:PARTS * D1].rearrange("p (i d) -> p d i", i=PARTS), AX, ALU.add).then_inc(sum_ready, 1)

            def keep(u, r, used, n):
                part = acc[:, bass.ds(step_value(dve, u, 0, WINDOWS - 1), 1), :].rearrange("p w d -> p (w d)")
                dve.wait_ge(sum_ready, u + 1)
                dve.wait_ge(acc_ready, u + 1)
                dve.tensor_tensor(part, part, step_sum[r % 2][:], ALU.add).then_inc(acc_ready, 1)

            staggered(dve, (make_rel, 0), (add, 3), (make_hot, 0), (relu_last, 3), (keep, 8), (add_parts, 7))
            dve.wait_ge(acc_ready, UNITS + 1)
            inverse_counts(dve, k, sum_ready, UNITS + 1)

        @block.tensor
        def _(pe):
            def turn(u, r, used, n):
                wait_alone(pe, hot_ready, u + 1)
                if n >= 2:
                    wait_alone(pe, hot_t_ready, u - 1)
                for t in range(UT):
                    mm = pe.transpose(hot_ps[r % 2][:, t, :], hot[r][:, t, :], k.ident_b[:])
                mm.then_inc(turned, 1)

            def expand(u, r, used, n):
                window = bass.ds(step_value(pe, u, 0, WINDOWS - 1), 1)
                pe.wait_ge(hot_t_ready, u + 1)
                if n >= 2:
                    pe.wait_ge(added, u - 1)
                for t in range(UT):
                    for i in range(PARTS):
                        mm = pe.matmul(a_ps[r % 2][:, t, :], hot_t[r % 2][:, t, :], k.a_parts[:, window, i, :].rearrange("p w d -> p (w d)"),
                                       start=(i == 0), stop=(i == PARTS - 1))
                mm.then_inc(expanded, 1)

            def sum_up(u, r, used, n):
                pe.wait_ge(third_ready, u + 1)
                if n >= 2:
                    pe.wait_ge(sum_ready, u - 1)
                for t in range(UT):
                    mm = pe.matmul(sums[r % 2][:, 0:PARTS * D1], hot[r][:, t, :], parts[r][:, t].rearrange("p i d -> p (i d)"), start=(t == 0), stop=(t == UT - 1))
                mm.then_inc(summed, 1)

            staggered(pe, (turn, 1), (expand, 2), (sum_up, 6))

        @block.scalar
        def _(act):
            act.wait_ge(parts_set, RING)

            def turn_back(u, r, used, n):
                act.wait_ge(turned, u + 1)
                if n >= 2:
                    act.wait_ge(expanded, u - 1)
                act.copy(hot_t[r % 2][:], hot_ps[r % 2][:]).then_inc(hot_t_ready, 1)

            def first_part(u, r, used, n):
                act.wait_ge(added, u + 1)
                if n >= RING:
                    act.wait_ge(summed, u - RING + 1)
                act.activation(parts[r][:, :, 0, 0:D], total[r % SHORT][:], ACT.Relu)
                if n >= SHORT:
                    act.wait_ge(third_ready, u - SHORT + 1)
                act.activation(left[r % SHORT][:, 0:ACT_T, :], total[r % SHORT][:, 0:ACT_T, :], ACT.Relu).then_inc(first_ready, 1)

            def second_part(u, r, used, n):
                act.wait_ge(left_ready, u + 1)
                act.copy(parts[r][:, :, 1, 0:D], left[r % SHORT][:]).then_inc(second_ready, 1)

            staggered(act, (first_part, 4), (second_part, 5), (turn_back, 1), rounds=2)

        @block.gpsimd
        def _(pool):
            pool.memset(acc[:], 0.0).then_inc(acc_ready, 1)

            def rest_of_first(u, r, used, n):
                pool.wait_ge(first_ready, u + 1)
                pool.wait_ge(last_ready, u + 1)
                pool.tensor_tensor(left[r % SHORT][:], left[r % SHORT][:], parts[r][:, :, 0, 0:D], ALU.subtract).then_inc(left_ready, 1)

            def third_part(u, r, used, n):
                pool.wait_ge(second_ready, u + 1)
                pool.tensor_tensor(parts[r][:, :, 2, 0:D], left[r % SHORT][:], parts[r][:, :, 1, 0:D], ALU.subtract).then_inc(third_ready, 1)

            staggered(pool, (rest_of_first, 4), (third_part, 5))


def add_bias(dve, k):
    dve.tensor_tensor(k.x[:], k.x[:], wide(k.conv_b[1][:], 1, [P, WINDOWS, D]), ALU.add)


def inverse_counts(dve, k, sem, value):
    link(dve, dve.tensor_scalar(k.inv_count[:], k.acc[:, 0:WINDOWS, D], 1.0, None, ALU.max), sem, value)
    dve.reciprocal(k.inv_count[:], k.inv_count[:])


def group(g):
    return bass.ds(g * GW, GW)


def program(nc, io, out):
    k = Core()
    shape = [P, GW, D]
    with ExitStack() as ctx:
        constants(nc, ctx, k)
        acc = k.acc

        def feed_norm(dve, stage, g, step):
            return dve.scalar_tensor_tensor(stage[:], k.centred[:, group(g), :], 0.0, wide(k.rstd[:, group(g)], 2, shape), ALU.max, ALU.mult)

        def keep_own(bias):
            def keep(dve, part, g, rows, step):
                return dve.tensor_tensor(k.own[:, group(g), :], part, wide(bias[:], 1, shape), ALU.add)
            return keep

        def feed_mean(dve, stage, g, step):
            link(dve, dve.tensor_tensor(stage[:], acc[:, group(g), 0:D], wide(k.inv_count[:, group(g)], 2, shape), ALU.mult), step, g + 1)
            return dve.tensor_tensor(stage[:], stage[:], k.own[:, group(g), :], ALU.add)

        def keep_x(dve, part, g, rows, step):
            return dve.tensor_tensor(k.x[:, group(g), :], k.x[:, group(g), :], part, ALU.add)

        def feed_sums(dve, stage, g, step):
            return dve.tensor_copy(stage[:], acc[:, group(g), :])

        def keep_out(dve, part, g, rows, step):
            link(dve, dve.tensor_tensor(rows[:], part, wide(k.inv_count[:, group(g)], 2, shape), ALU.mult), step, g + 1)
            return dve.tensor_tensor(rows[:], rows[:], k.x[:, group(g), :], ALU.add)

        with nc.sbuf_tensor("own_part", [P, WINDOWS, D], F32) as k.own:
            with nc.sbuf_tensor("centred", [P, WINDOWS, D], F32) as k.centred:
                setup(nc, k, io)
                project(nc, k, "conv1_in", D, k.conv_w[0], feed_norm, False, k.h_table, keep_own(k.conv_b[0]))
                sum_by_dst(nc, k, "agg1", k.h_table, acc, lambda dve: add_bias(dve, k), Counting)
                project(nc, k, "conv2_in", D, k.conv_w[1], feed_mean, True, k.g_table, keep_x, steps=True)
                sum_by_dst(nc, k, "agg2", k.g_table, acc, lambda dve: None, Ranking)
                second_norm(nc, k, acc)
                project(nc, k, "edge_in", D, k.edge_ends, feed_norm, False, k.b_table, keep_own(k.edge_b1))
            place_edges(nc, k, io["edge_attr_64"])
        sum_by_src(nc, k, acc)
        project(nc, k, "edge_out", D1, k.edge_out, feed_sums, False, None, keep_out, steps=True, out=out)


INS = ["x", "src", "dst", "edge_attr_64", "L0_gnn_W1l", "L0_gnn_W1r", "L0_gnn_b1", "L0_gnn_W2l", "L0_gnn_W2r", "L0_gnn_b2",
       "L1_gnn_W1", "L1_gnn_b1", "L1_gnn_W2", "L1_gnn_b2"]


def kernel(**inputs):
    import numpy as np
    import concourse.bacc as bacc
    from concourse import mybir as mb
    from concourse.bass_utils import run_bass_kernel_spmd

    nc = bacc.Bacc("TRN2", target_bir_lowering=False, num_devices=1)
    arrays, io = {}, {}
    for name in INS:
        a = np.ascontiguousarray(inputs[name])
        arrays[f"in_{name}"] = a
        io[name] = nc.dram_tensor(f"in_{name}", a.shape, mb.dt.from_np(a.dtype), kind="ExternalInput").ap()
    out = nc.dram_tensor("out_0", (N, D), mb.dt.float32, kind="ExternalOutput").ap()
    program(nc, io, out)
    r = run_bass_kernel_spmd(nc, [arrays], core_ids=[0])
    return r.results[0]["out_0"]
```
